# Optimizing a Trainium2 kernel written in Bass

```python
import numpy as np
import jax
import jax.numpy as jnp

def _softmax(x, axis=-1):
    return jax.nn.softmax(x, axis=axis)

def _gelu(x):
    return jax.nn.gelu(x, approximate=True)

def _silu(x):
    return jax.nn.silu(x)

def _sigmoid(x):
    return jax.nn.sigmoid(x)

def _layernorm(x, axis=-1, eps=1e-05):
    m = jnp.mean(x, axis=axis, keepdims=True)
    v = jnp.var(x, axis=axis, keepdims=True)
    return (x - m) / jnp.sqrt(v + eps)

def _scatter_add(tgt, idx, src, axis=0):
    return tgt.at[idx].add(src)

def _segment_sum(src, seg, n):
    return jax.ops.segment_sum(src, seg, n)
kernel_name = 'mk_adaln_d1_jaxref_r4_69b49a'

def setup_inputs(seed: int=0):
    np.random.seed(seed)
    _w = jnp.asarray

    def _L0_attn_setup():
        import jax, jax.numpy as jnp
        import numpy as np
        D_MODEL = 256
        HEAD_DIM = 64
        CHUNK = 64
        N_HEADS = D_MODEL // HEAD_DIM
        MEM_ALPHA = 0.03

        def _forward(out, Ww, Wr, decay, log_alpha):
            B, T, D = out.shape
            H, d, C = (N_HEADS, HEAD_DIM, CHUNK)
            x = out.astype(jnp.float32)
            gamma = jax.nn.sigmoid(decay)
            log_gamma = jnp.log(gamma)
            v = (x @ Ww.T).reshape(B, T, H, d).transpose(0, 2, 1, 3)
            xh = x.reshape(B, T, H, d)
            rk = xh / jnp.maximum(jnp.linalg.norm(xh, axis=-1, keepdims=True), 1e-12)
            rk = rk.transpose(0, 2, 1, 3)
            wk = jnp.concatenate([jnp.zeros((B, H, 1, d), jnp.float32), rk[:, :, :-1]], axis=2)
            BH = B * H
            gamma_bh = jnp.tile(gamma, B)
            log_gamma_bh = jnp.tile(log_gamma, B)
            v = v.reshape(BH, T, d)
            rk = rk.reshape(BH, T, d)
            wk = wk.reshape(BH, T, d)
            pad = -T % C
            if pad:
                z = ((0, 0), (0, pad), (0, 0))
                v, rk, wk = (jnp.pad(v, z), jnp.pad(rk, z), jnp.pad(wk, z))
            T_pad = T + pad
            N = T_pad // C
            v = v.reshape(BH, N, C, d)
            rk = rk.reshape(BH, N, C, d)
            wk = wk.reshape(BH, N, C, d)
            p = jnp.arange(C)
            diffs = jnp.maximum(p[:, None] - p[None, :], 0).astype(jnp.float32)
            L = jnp.tril(jnp.exp(diffs * log_gamma_bh[:, None, None]))
            strict = jnp.tril(jnp.ones((C, C), bool), -1)
            A0 = -jnp.where(strict, jnp.einsum('bnid,bnjd->bnij', wk, wk) * L[:, None], 0.0)
            eye = jnp.eye(C, dtype=jnp.float32)
            A = jnp.linalg.inv(eye - A0)
            gp = gamma_bh[:, None, None] ** p[None, :, None]
            gp_tail = gamma_bh[:, None, None] ** (C - 1 - p)[None, :, None]
            gamma_C = (gamma_bh ** C)[:, None, None]
            intra = jnp.where(strict, jnp.einsum('bnid,bnjd->bnij', rk, wk) * L[:, None], 0.0)
            rk_g = rk * gp[:, None]
            wk_g = (wk * gp_tail[:, None]).transpose(0, 1, 3, 2)

            def step(S, inp):
                A_i, v_i, wk_i, rkg_i, wkg_i, intra_i = inp
                v_corr = A_i @ v_i
                wk_corr = A_i @ wk_i
                v_new = v_corr - wk_corr @ S
                o_i = rkg_i @ S + intra_i @ v_new
                S = gamma_C * S + wkg_i @ v_new
                return (S, o_i)
            mv = lambda a: jnp.moveaxis(a, 1, 0)
            S0 = jnp.zeros((BH, d, d), jnp.float32)
            _, o = jax.lax.scan(step, S0, (mv(A), mv(v), mv(wk), mv(rk_g), mv(wk_g), mv(intra)))
            o = jnp.moveaxis(o, 0, 1).reshape(B, H, T_pad, d)
            alpha = jnp.exp(log_alpha)[None, :, None, None]
            o = (alpha * o).transpose(0, 2, 1, 3).reshape(B, T_pad, D)[:, :T]
            return out + (o @ Wr.T).astype(out.dtype)
        key = jax.random.key(seed)
        k0, k1, k2 = jax.random.split(key, 3)
        B, T = (2, 2048)
        out = jax.random.normal(k0, (B, T, D_MODEL), jnp.float32)
        Ww = jax.random.normal(k1, (D_MODEL, D_MODEL), jnp.float32) * 0.02
        Wr = jax.random.normal(k2, (D_MODEL, D_MODEL), jnp.float32) * 0.02
        decay = jnp.full((N_HEADS,), 4.6, jnp.float32)
        log_alpha = jnp.log(jnp.full((N_HEADS,), MEM_ALPHA, jnp.float32))
        return {'out': out, 'Ww': Ww, 'Wr': Wr, 'decay': decay, 'log_alpha': log_alpha}
    _L0_attn_in = _L0_attn_setup()

    def _L0_ffn_setup():
        import jax, jax.numpy as jnp
        import numpy as np
        D_IN, D_HID = (256, 1024)

        def _ternary(key, shape):
            return jax.random.randint(key, shape, -1, 2).astype(jnp.float32)

        def _tlin(x, w, s):
            return jnp.einsum('bsi,oi->bso', x, w) * s
        key = jax.random.key(seed)
        ks = jax.random.split(key, 12)
        inv = lambda fan: 1.0 / np.sqrt(fan).astype(np.float32)
        return {'x': jax.random.normal(ks[0], (4, 512, D_IN), dtype=jnp.float32), 'w1_w': _ternary(ks[1], (D_HID, D_IN)), 'w1_s': jax.random.uniform(ks[2], (D_HID,), dtype=jnp.float32) * inv(D_IN), 'w2_w': _ternary(ks[3], (D_HID, D_IN)), 'w2_s': jax.random.uniform(ks[4], (D_HID,), dtype=jnp.float32) * inv(D_IN), 'h1_w': _ternary(ks[5], (D_HID, D_HID)), 'h1_s': jax.random.uniform(ks[6], (D_HID,), dtype=jnp.float32) * inv(D_HID), 'h2_w': _ternary(ks[7], (D_HID, D_HID)), 'h2_s': jax.random.uniform(ks[8], (D_HID,), dtype=jnp.float32) * inv(D_HID), 'w3_w': _ternary(ks[9], (D_IN, D_HID)), 'w3_s': jax.random.uniform(ks[10], (D_IN,), dtype=jnp.float32) * inv(D_HID)}
    _L0_ffn_in = _L0_ffn_setup()
    _L0_c = _w((lambda *s: np.random.randn(*s).astype(np.float32) * 0.05)(4, 256))
    _L0_wmod = _w((lambda *s: np.random.randn(*s).astype(np.float32) * 0.05)(256, 6 * 256) * 256 ** (-0.5))
    _d = {'L0_attn_out': _L0_attn_in['out'], 'L0_attn_Ww': _L0_attn_in['Ww'], 'L0_attn_Wr': _L0_attn_in['Wr'], 'L0_attn_decay': _L0_attn_in['decay'], 'L0_attn_log_alpha': _L0_attn_in['log_alpha'], 'L0_ffn_w1_w': _L0_ffn_in['w1_w'], 'L0_ffn_w1_s': _L0_ffn_in['w1_s'], 'L0_ffn_w2_w': _L0_ffn_in['w2_w'], 'L0_ffn_w2_s': _L0_ffn_in['w2_s'], 'L0_ffn_h1_w': _L0_ffn_in['h1_w'], 'L0_ffn_h1_s': _L0_ffn_in['h1_s'], 'L0_ffn_h2_w': _L0_ffn_in['h2_w'], 'L0_ffn_h2_s': _L0_ffn_in['h2_s'], 'L0_ffn_w3_w': _L0_ffn_in['w3_w'], 'L0_ffn_w3_s': _L0_ffn_in['w3_s'], 'L0_c': _L0_c, 'L0_wmod': _L0_wmod}
    _x0 = _d['L0_attn_out']
    _d['L0_attn_out'] = jax.random.normal(jax.random.fold_in(jax.random.key(seed), 1), (4, 2048, 256), dtype=_x0.dtype)
    del _x0
    return _d

def reference(L0_attn_out, L0_attn_Ww, L0_attn_Wr, L0_attn_decay, L0_attn_log_alpha, L0_ffn_w1_w, L0_ffn_w1_s, L0_ffn_w2_w, L0_ffn_w2_s, L0_ffn_h1_w, L0_ffn_h1_s, L0_ffn_h2_w, L0_ffn_h2_s, L0_ffn_w3_w, L0_ffn_w3_s, L0_c, L0_wmod):

    def _L0_attn_ref(out, Ww, Wr, decay, log_alpha):
        import jax, jax.numpy as jnp
        import numpy as np
        D_MODEL = 256
        HEAD_DIM = 64
        CHUNK = 64
        N_HEADS = D_MODEL // HEAD_DIM
        MEM_ALPHA = 0.03

        def _forward(out, Ww, Wr, decay, log_alpha):
            B, T, D = out.shape
            H, d, C = (N_HEADS, HEAD_DIM, CHUNK)
            x = out.astype(jnp.float32)
            gamma = jax.nn.sigmoid(decay)
            log_gamma = jnp.log(gamma)
            v = (x @ Ww.T).reshape(B, T, H, d).transpose(0, 2, 1, 3)
            xh = x.reshape(B, T, H, d)
            rk = xh / jnp.maximum(jnp.linalg.norm(xh, axis=-1, keepdims=True), 1e-12)
            rk = rk.transpose(0, 2, 1, 3)
            wk = jnp.concatenate([jnp.zeros((B, H, 1, d), jnp.float32), rk[:, :, :-1]], axis=2)
            BH = B * H
            gamma_bh = jnp.tile(gamma, B)
            log_gamma_bh = jnp.tile(log_gamma, B)
            v = v.reshape(BH, T, d)
            rk = rk.reshape(BH, T, d)
            wk = wk.reshape(BH, T, d)
            pad = -T % C
            if pad:
                z = ((0, 0), (0, pad), (0, 0))
                v, rk, wk = (jnp.pad(v, z), jnp.pad(rk, z), jnp.pad(wk, z))
            T_pad = T + pad
            N = T_pad // C
            v = v.reshape(BH, N, C, d)
            rk = rk.reshape(BH, N, C, d)
            wk = wk.reshape(BH, N, C, d)
            p = jnp.arange(C)
            diffs = jnp.maximum(p[:, None] - p[None, :], 0).astype(jnp.float32)
            L = jnp.tril(jnp.exp(diffs * log_gamma_bh[:, None, None]))
            strict = jnp.tril(jnp.ones((C, C), bool), -1)
            A0 = -jnp.where(strict, jnp.einsum('bnid,bnjd->bnij', wk, wk) * L[:, None], 0.0)
            eye = jnp.eye(C, dtype=jnp.float32)
            A = jnp.linalg.inv(eye - A0)
            gp = gamma_bh[:, None, None] ** p[None, :, None]
            gp_tail = gamma_bh[:, None, None] ** (C - 1 - p)[None, :, None]
            gamma_C = (gamma_bh ** C)[:, None, None]
            intra = jnp.where(strict, jnp.einsum('bnid,bnjd->bnij', rk, wk) * L[:, None], 0.0)
            rk_g = rk * gp[:, None]
            wk_g = (wk * gp_tail[:, None]).transpose(0, 1, 3, 2)

            def step(S, inp):
                A_i, v_i, wk_i, rkg_i, wkg_i, intra_i = inp
                v_corr = A_i @ v_i
                wk_corr = A_i @ wk_i
                v_new = v_corr - wk_corr @ S
                o_i = rkg_i @ S + intra_i @ v_new
                S = gamma_C * S + wkg_i @ v_new
                return (S, o_i)
            mv = lambda a: jnp.moveaxis(a, 1, 0)
            S0 = jnp.zeros((BH, d, d), jnp.float32)
            _, o = jax.lax.scan(step, S0, (mv(A), mv(v), mv(wk), mv(rk_g), mv(wk_g), mv(intra)))
            o = jnp.moveaxis(o, 0, 1).reshape(B, H, T_pad, d)
            alpha = jnp.exp(log_alpha)[None, :, None, None]
            o = (alpha * o).transpose(0, 2, 1, 3).reshape(B, T_pad, D)[:, :T]
            return out + (o @ Wr.T).astype(out.dtype)
        return _forward(out, Ww, Wr, decay, log_alpha)

    def _L0_ffn_ref(x, w1_w, w1_s, w2_w, w2_s, h1_w, h1_s, h2_w, h2_s, w3_w, w3_s):
        import jax, jax.numpy as jnp
        import numpy as np
        D_IN, D_HID = (256, 1024)

        def _ternary(key, shape):
            return jax.random.randint(key, shape, -1, 2).astype(jnp.float32)

        def _tlin(x, w, s):
            return jnp.einsum('bsi,oi->bso', x, w) * s
        h = jax.nn.silu(_tlin(x, w1_w, w1_s)) * _tlin(x, w2_w, w2_s)
        h = jax.nn.gelu(_tlin(h, h1_w, h1_s), approximate=False)
        h = jax.nn.gelu(_tlin(h, h2_w, h2_s), approximate=False)
        return _tlin(h, w3_w, w3_s)
    x = L0_attn_out
    mod = (_silu(L0_c) @ L0_wmod).reshape(L0_c.shape[0], 6, 1, -1)
    sa, ca, ga, sb, cb, gb = (mod[:, 0], mod[:, 1], mod[:, 2], mod[:, 3], mod[:, 4], mod[:, 5])
    ga = (2 * (ga >= 0) - 1) * jnp.maximum(jnp.abs(ga), 0.25)
    gb = (2 * (gb >= 0) - 1) * jnp.maximum(jnp.abs(gb), 0.25)
    h = _layernorm(x, axis=-1) * (1 + ca) + sa
    x = x + ga * _L0_attn_ref(h, L0_attn_Ww, L0_attn_Wr, L0_attn_decay, L0_attn_log_alpha)
    h = _layernorm(x, axis=-1) * (1 + cb) + sb
    x = x + gb * _L0_ffn_ref(h, L0_ffn_w1_w, L0_ffn_w1_s, L0_ffn_w2_w, L0_ffn_w2_s, L0_ffn_h1_w, L0_ffn_h1_s, L0_ffn_h2_w, L0_ffn_h2_s, L0_ffn_w3_w, L0_ffn_w3_s)
    return x

_drawn_inputs = setup_inputs


def setup_inputs(seed=0):
    import zlib

    import numpy as np

    out = dict(_drawn_inputs(seed))
    spreads = {'L0_attn_decay': (4.599999904632568, 0.2), 'L0_attn_log_alpha': (-3.5065579414367676, 0.2)}
    factors = {}
    for name, (base, spread) in spreads.items():
        noise = np.random.default_rng([zlib.crc32(name.encode()), seed]).standard_normal(out[name].shape)
        drawn = base * np.exp(spread * noise) if base else spread * noise
        out[name] = jnp.asarray(drawn.astype(out[name].dtype))
    for name, factor in factors.items():
        out[name] = (out[name] * factor).astype(out[name].dtype)
    return out
```

```python
from contextlib import ExitStack

import numpy as np

import concourse.bass as bass
from concourse import mybir

F32 = mybir.dt.float32
F32R = mybir.dt.float32r
I32 = mybir.dt.int32
ACT = mybir.ActivationFunctionType
ALU = mybir.AluOpType
AX = mybir.AxisListType

P = 128
B, T, D = 4, 2048, 256
H, DH, C = 4, 64, 64
HID = 1024
KT = D // P
HK = HID // P
NB = 2
NG = B // NB
NP = NB * (H // 2)
STEPS = (T // P) * NG
TOK = NB * P
LEVELS = 6
EPS = 1e-5

BLK_W1, BLK_W2 = 0, HK * KT
BLK_H1 = BLK_W2 + HK * KT
BLK_H2 = BLK_H1 + HK * HK
BLK_W3 = BLK_H2 + HK * HK
BLOCKS = BLK_W3 + HK * KT
SLOT = 8
SLOTS = BLOCKS // SLOT

CO_ID, CO_EYE = 0, P
CO_MASK = CO_EYE + C
CO_UP = CO_MASK + LEVELS * C
CO_DIST = CO_UP + C
CO_POS = CO_DIST + C
CO_TAIL = CO_POS + C
CO_E = CO_TAIL + 1
CO_N = CO_E + 1


def constants():
    c = np.zeros((P, CO_N), np.float32)
    p = np.arange(P)[:, None]
    j, i = p % C, np.arange(C)[None, :]
    c[:, CO_ID:CO_ID + P] = np.eye(P)
    c[:, CO_EYE:CO_EYE + C] = j == i
    c[:, CO_MASK:CO_MASK + C] = -1.0 * ((j >> 1 == i >> 1) & (j > i))
    for k in range(1, LEVELS):
        c[:, CO_MASK + k * C:CO_MASK + (k + 1) * C] = (
            (j >> (k + 1) == i >> (k + 1)) & ((i >> k) % 2 == 1) & ((j >> k) % 2 == 0))
    c[:, CO_UP:CO_UP + C] = i > j
    c[:, CO_DIST:CO_DIST + C] = np.abs(i - j)
    c[:, CO_POS:CO_POS + C] = i
    c[:, CO_TAIL] = C - 1 - j[:, 0]
    c[:, CO_E] = np.e
    return c


def half(k):
    return slice(C * k, C * k + C)


def adaln_block(nc, x, wts, wv, wr, wmod, cT, cB, scales, s3, dec_pair, dec_all, alpha_pair, const, out):
    low_dram = nc.dram_tensor("low_parts", (SLOTS, P, SLOT * P), F32, kind="Internal").ap()
    with ExitStack() as ctx:
        def sb(name, shape, dt=F32, c=ctx):
            return c.enter_context(nc.sbuf_tensor(name, [P] + list(shape), dt))

        def sem(name):
            return ctx.enter_context(nc.semaphore(name))

        def sems(name, n):
            return [sem(f"{name}{i}") for i in range(n)]

        duo = [ctx.enter_context(nc.psum_tensor(f"duo{i}", [P, 2, 512], F32)) for i in range(2)]
        solo = [ctx.enter_context(nc.psum_tensor(f"solo{i}", [P, 512], F32)) for i in range(2)]
        mlp = [ctx.enter_context(nc.psum_tensor(f"mlp{i}", [P, 512], F32)) for i in range(2)]

        w_hi = sb("w_hi", [BLOCKS, P], F32R)
        wv_sb = sb("wv_sb", [KT, D])
        wr_sb = sb("wr_sb", [KT, D])
        con = sb("con", [CO_N])
        scale_sb = sb("scale_sb", [4, HK])
        ca1 = sb("ca1", [B, D])
        sa = sb("sa", [B, D])
        ga = sb("ga", [B, D])
        gbs = sb("gbs", [B, D])
        cb1 = sb("cb1", [KT, B])
        sbm = sb("sbm", [KT, B])
        level_mask = sb("level_mask", [LEVELS, H // 2, 2, C])
        intra_mask = sb("intra_mask", [2, H // 2, C])
        head_decay = sb("head_decay", [H // 2, 2, C])
        tail_decay = sb("tail_decay", [H])
        chunk_decay = sb("chunk_decay", [H // 2])
        minus_half = sb("minus_half", [NB * H])
        flag_i = sb("flag_i", [1], I32)
        state = [sb(f"state{g}", [NP, DH]) for g in range(NG)]
        rT = [sb(f"rT{g}", [NP, P + 1]) for g in range(NG)]

        const_in, small_in, wst_in, low_out = sem("const_in"), sem("small_in"), sems("wst_in", 2), sems("low_out", 2)
        hi_done, lo_done, max_done = sem("hi_done"), sem("lo_done"), sem("max_done")
        flag_col, flag_row, flag_max, flag_set = sem("flag_col"), sem("flag_row"), sem("flag_max"), sem("flag_set")
        pool_set, dve_set, act_set, pe_set = sem("pool_set"), sem("dve_set"), sem("act_set"), sem("pe_set")

        with ExitStack() as tmp:
            wst = [sb(f"wst{i}", [SLOT * P], F32, tmp) for i in range(2)]
            lost = [sb(f"lost{i}", [SLOT * P], F32, tmp) for i in range(2)]
            wmod_sb = sb("wmod_sb", [KT, 6 * D], F32, tmp)
            cT_sb = sb("cT_sb", [KT, B], F32, tmp)
            cB_sb = sb("cB_sb", [KT, B, P], F32, tmp)
            scT = sb("scT", [KT, B], F32, tmp)
            scB = sb("scB", [KT, B, P], F32, tmp)
            s3_sb = sb("s3_sb", [D], F32, tmp)
            dec = sb("dec", [H // 2 + H + H // 2], F32, tmp)
            gam = sb("gam", [H // 2 + H + H // 2], F32, tmp)
            edec = sb("edec", [H // 2 + H + H // 2], F32, tmp)
            dist_pow = sb("dist_pow", [H // 2, C], F32, tmp)
            all_pow = sb("all_pow", [H, C], F32, tmp)
            pos_pow = sb("pos_pow", [H // 2, C], F32, tmp)
            sgn = sb("sgn", [2, B, D], F32, tmp)
            mag = sb("mag", [2, B, D], F32, tmp)
            slot_max = sb("slot_max", [SLOTS], F32, tmp)
            low_max = sb("low_max", [1], F32, tmp)
            low_any = sb("low_any", [1], F32, tmp)
            NPAIR = H // 2
            DEC_PAIR, DEC_ALL, DEC_ALPHA = slice(0, NPAIR), slice(NPAIR, NPAIR + H), slice(NPAIR + H, NPAIR + H + NPAIR)

            with nc.Block() as block:
                @block.sync
                def _(sp):
                    sp.dma_start(con[:], const).then_inc(const_in, 16)
                    sp.dma_start(dec[:, DEC_PAIR], dec_pair).then_inc(const_in, 16)
                    sp.dma_start(dec[:, DEC_ALL], dec_all).then_inc(const_in, 16)
                    sp.dma_start(dec[:, DEC_ALPHA], alpha_pair).then_inc(const_in, 16)
                    for s in range(2):
                        sp.dma_start(wst[s][:], wts[s]).then_inc(wst_in[s], 16)
                    def store_low(slot, s):
                        row = low_dram[slot] if isinstance(slot, int) else low_dram[bass.ds(slot, 1)].rearrange("a p n -> (a p) n")
                        sp.dma_start(row, lost[s][:]).then_inc(low_out[s], 16)

                    with sp.Fori(1, SLOTS // 2) as i:
                        for s in range(2):
                            sp.wait_ge(lo_done, 2 * i + s - 1)
                            sp.dma_start(wst[s][:], wts[bass.ds(2 * i + s, 1)].rearrange("a p n -> (a p) n")).then_inc(wst_in[s], 16)
                            store_low(2 * i + s - 2, s)
                    for s in range(2):
                        sp.wait_ge(lo_done, SLOTS - 1 + s)
                        store_low(SLOTS - 2 + s, s)
                    for s in range(2):
                        sp.wait_ge(low_out[s], 16 * (SLOTS // 2))

                @block.scalar
                def _(act):
                    for dst, src in ((cT_sb, cT), (cB_sb, cB), (wmod_sb, wmod), (s3_sb, s3), (scale_sb, scales),
                                     (wv_sb, wv), (wr_sb, wr)):
                        act.dma_start(dst[:], src).then_inc(small_in, 16)
                    act.wait_ge(small_in, 7 * 16)
                    act.activation(scT[:], cT_sb[:], ACT.Silu).then_inc(act_set, 1)
                    act.activation(scB[:], cB_sb[:], ACT.Silu).then_inc(act_set, 1)
                    with act.Fori(0, SLOTS // 2) as i:
                        for s in range(2):
                            act.wait_ge(wst_in[s], 16 * i + 16)
                            act.copy(w_hi[:, bass.ds(SLOT * (2 * i + s), SLOT), :],
                                     wst[s][:].rearrange("p (b n) -> p b n", n=P)).then_inc(hi_done, 1)

                @block.gpsimd
                def _(pool):
                    pool.memset(minus_half[:], -0.5).then_inc(pool_set, 1)
                    for g in range(NG):
                        pool.memset(state[g][:], 0.0)
                        pool.memset(rT[g][:], 0.0).then_inc(pool_set, 1)
                    pool.wait_ge(const_in, 64)
                    pool.tensor_scalar(edec[:, 0:NPAIR + H], dec[:, 0:NPAIR + H], -1.0, None, ALU.mult).then_inc(pool_set, 1)
                    pool.tensor_copy(edec[:, DEC_ALPHA], dec[:, DEC_ALPHA]).then_inc(pool_set, 1)
                    pool.wait_ge(pool_set, 5)
                    pool.tensor_tensor(gam[:], con[:, CO_E:CO_E + 1].to_broadcast([P, 2 * NPAIR + H]), edec[:], ALU.pow).then_inc(pool_set, 1)
                    pool.wait_ge(dve_set, 2)
                    for h in range(NPAIR):
                        pool.tensor_tensor(dist_pow[:, h, :], gam[:, h:h + 1].to_broadcast([P, C]), con[:, CO_DIST:CO_DIST + C], ALU.pow)
                        pool.tensor_tensor(pos_pow[:, h, :], gam[:, h:h + 1].to_broadcast([P, C]), con[:, CO_POS:CO_POS + C], ALU.pow)
                    for h in range(H):
                        g_h = gam[:, NPAIR + h:NPAIR + h + 1]
                        pool.tensor_tensor(all_pow[:, h, :], g_h.to_broadcast([P, C]), con[:, CO_DIST:CO_DIST + C], ALU.pow)
                        pool.tensor_tensor(tail_decay[:, h:h + 1], g_h, con[:, CO_TAIL:CO_TAIL + 1], ALU.pow)
                    pool.memset(chunk_decay[:], float(C)).then_inc(pool_set, 1)
                    pool.wait_ge(pool_set, 7)
                    pool.tensor_tensor(chunk_decay[:], gam[:, DEC_PAIR], chunk_decay[:], ALU.pow).then_inc(pool_set, 1)

                @block.vector
                def _(dve):
                    dve.wait_ge(pool_set, 6)
                    dve.tensor_scalar(gam[:, 0:NPAIR + H], gam[:, 0:NPAIR + H], 1.0, None, ALU.add).then_inc(dve_set, 1)
                    dve.wait_ge(dve_set, 1)
                    dve.reciprocal(gam[:, 0:NPAIR + H], gam[:, 0:NPAIR + H]).then_inc(dve_set, 1)
                    dve.wait_ge(small_in, 7 * 16)
                    for h in range(NPAIR):
                        dve.tensor_scalar(wr_sb[:, h, :], wr_sb[:, h, :], gam[:, NPAIR + H + h:NPAIR + H + h + 1], None, ALU.mult)
                    for b in range(B):
                        lo_bank, hi_bank = duo[b % 2][:, 0, :], duo[b % 2][:, 1, :]
                        dve.wait_ge(pe_set, b + 1)
                        dve.tensor_copy(sa[:, b, :], lo_bank[:, 0:D])
                        dve.tensor_scalar(ca1[:, b, :], lo_bank[:, D:2 * D], 1.0, None, ALU.add)
                        dve.tensor_copy(ga[:, b, :], hi_bank[:, 0:D])
                        dve.tensor_copy(gbs[:, b, :], hi_bank[:, D:2 * D]).then_inc(dve_set, 1)
                    dve.wait_ge(pe_set, B + 1)
                    for k in range(KT):
                        dve.tensor_copy(sbm[:, k, :], mlp[0][:, B * k:B * k + B])
                        dve.tensor_scalar(cb1[:, k, :], mlp[0][:, B * (KT + k):B * (KT + k + 1)], 1.0, None, ALU.add)
                    dve.wait_ge(dve_set, 2 + B)
                    for k, g in enumerate((ga, gbs)):
                        dve.tensor_scalar(sgn[:, k], g[:], 0.0, 2.0, ALU.is_ge, ALU.mult)
                        dve.scalar_tensor_tensor(mag[:, k], g[:], -1.0, g[:], ALU.mult, ALU.max).then_inc(dve_set, 1)
                    dve.wait_ge(dve_set, 4 + B)
                    for k in range(2):
                        dve.tensor_scalar(sgn[:, k], sgn[:, k], -1.0, None, ALU.add)
                        dve.tensor_scalar(mag[:, k], mag[:, k], 0.25, None, ALU.max).then_inc(dve_set, 1)
                    dve.wait_ge(dve_set, 6 + B)
                    dve.tensor_tensor(ga[:], mag[:, 0], sgn[:, 0], ALU.mult)
                    dve.tensor_tensor(gbs[:], mag[:, 1], sgn[:, 1], ALU.mult).then_inc(dve_set, 1)
                    dve.wait_ge(dve_set, 7 + B)
                    for b in range(B):
                        dve.tensor_tensor(gbs[:, b, :], gbs[:, b, :], s3_sb[:], ALU.mult)
                    dve.wait_ge(pool_set, 8)
                    for k in range(LEVELS):
                        m = con[:, CO_MASK + k * C:CO_MASK + (k + 1) * C]
                        for h in range(NPAIR):
                            for c in range(2):
                                dve.tensor_tensor(level_mask[:, k, h, c, :], dist_pow[:, h, :], m, ALU.mult)
                    for h in range(NPAIR):
                        for c in range(2):
                            dve.tensor_tensor(intra_mask[:, c, h, :], all_pow[:, 2 * h + c, :], con[:, CO_UP:CO_UP + C], ALU.mult)
                            dve.tensor_copy(head_decay[:, h, c, :], pos_pow[:, h, :])
                    def low_part(s, i, first):
                        dve.wait_ge(hi_done, 2 * i + s + 1)
                        if not first:
                            dve.wait_ge(low_out[s], 16 * i)
                        dve.tensor_tensor(lost[s][:], wst[s][:],
                                          w_hi[:, bass.ds(SLOT * (2 * i + s), SLOT), :].bitcast(F32).rearrange("p b n -> p (b n)"),
                                          ALU.subtract).then_inc(lo_done, 1)
                        dve.wait_ge(lo_done, 2 * i + s + 1)
                        dve.tensor_reduce(slot_max[:, bass.ds(2 * i + s, 1)], lost[s][:], AX.X, ALU.max,
                                          apply_absolute_value=True).then_inc(max_done, 1)
                    for s in range(2):
                        low_part(s, 0, True)
                    with dve.Fori(1, SLOTS // 2) as i:
                        for s in range(2):
                            low_part(s, i, False)
                    dve.wait_ge(max_done, SLOTS)
                    dve.tensor_reduce(low_max[:], slot_max[:], AX.X, ALU.max).then_inc(flag_col, 1)
                    dve.wait_ge(flag_row, 1)
                    dve.tensor_reduce(low_any[0:1, :], mlp[1][0:1, 0:P], AX.X, ALU.max).then_inc(flag_max, 1)
                    dve.wait_ge(flag_max, 1)
                    dve.tensor_scalar(flag_i[0:1, :], low_any[0:1, :], 0.0, None, ALU.is_gt).then_inc(flag_set, 1)

                @block.tensor
                def _(pe):
                    pe.wait_ge(act_set, 2)
                    for b in range(B):
                        lo_bank, hi_bank = duo[b % 2][:, 0, :], duo[b % 2][:, 1, :]
                        if b >= 2:
                            pe.wait_ge(dve_set, 2 + b - 1)
                        for dst, col, n in ((lo_bank, 0, 2 * D), (hi_bank[:, 0:D], 2 * D, D), (hi_bank[:, D:2 * D], 5 * D, D)):
                            for k in range(KT):
                                mm = pe.matmul(dst, scB[:, k, b, :], wmod_sb[:, k, col:col + n], start=k == 0, stop=k == KT - 1)
                        mm.then_inc(pe_set, 1)
                    for q in range(2 * KT):
                        for k in range(KT):
                            mm = pe.matmul(mlp[0][:, B * q:B * q + B], wmod_sb[:, k, 3 * D + q * P:3 * D + (q + 1) * P],
                                           scT[:, k, :], start=k == 0, stop=k == KT - 1)
                    mm.then_inc(pe_set, 1)
                    pe.wait_ge(flag_col, 1)
                    pe.transpose(mlp[1][0:1, 0:P], low_max[:], con[:, CO_ID:CO_ID + P]).then_inc(flag_row, 1)

        main(nc, ctx, sb, sem, sems, locals())


def main(nc, ctx, sb, sem, sems, env):
    (x, out, duo, solo, mlp, w_hi, wv_sb, wr_sb, con, scale_sb, ca1, sa, ga, gbs, cb1, sbm, level_mask, intra_mask,
     head_decay, tail_decay, chunk_decay, minus_half, flag_i, state, rT, low_dram) = (env[k] for k in (
        "x", "out", "duo", "solo", "mlp", "w_hi", "wv_sb", "wr_sb", "con", "scale_sb", "ca1", "sa", "ga", "gbs", "cb1", "sbm",
        "level_mask", "intra_mask", "head_decay", "tail_decay", "chunk_decay", "minus_half", "flag_i", "state", "rT",
        "low_dram"))
    flag_set, flag_row = env["flag_set"], env["flag_row"]
    ident = con[:, CO_ID:CO_ID + P]

    xin = sb("xin", [NB, D])
    st1 = sb("st1", [NB, 6])
    mv1 = sb("mv1", [NB, 2])
    ve1 = sb("ve1", [NB])
    rstd1 = sb("rstd1", [NB])
    h = sb("h", [NB, D])
    r = sb("r", [NB, D])
    ss = sb("ss", [NB * H])
    ssm = sb("ssm", [NB * H])
    rinv = sb("rinv", [NB * H])
    gah = sb("gah", [NB, D])
    base = sb("base", [NB, D])
    hT = sb("hT", [KT, NB, P])
    v = sb("v", [NB, D])
    kg = sb("kg", [NP, 2, DH])
    gram = sb("gram", [NP, 2, C])
    intra = sb("intra", [2, NP, C])
    rg = sb("rg", [NP, P])
    lv = [sb(f"lv{i}", [NP, 2, C]) for i in range(2)]
    inv = sb("inv", [NP, 2, C])
    invT = sb("invT", [NP, 2, C])
    mi = sb("mi", [2, NP, C])
    vn = sb("vn", [NP, 2, DH])
    o_state = sb("o_state", [NP, P])
    oT = sb("oT", [NP, P])
    x1 = [sb(f"x1_{i}", [NB, D]) for i in range(2)]
    st2 = sb("st2", [NB, 6])
    mv2 = sb("mv2", [NB, 2])
    ve2 = sb("ve2", [NB])
    rstd2 = sb("rstd2", [NB])
    xn2 = sb("xn2", [NB, D])
    h2 = sb("h2", [KT, NB, P])
    xh = sb("xh", [KT, TOK], F32R)
    xl = sb("xl", [KT, TOK], F32R)
    act_hi = [sb(f"act_hi{i}", [HK, TOK], F32R) for i in range(2)]
    act_lo = [sb(f"act_lo{i}", [HK, TOK], F32R) for i in range(2)]
    gate = [sb(f"gate{i}", [TOK]) for i in range(2)]
    full = [sb(f"full{i}", [TOK]) for i in range(2)]
    y = sb("y", [NB, D])
    low = sb("low", [SLOT, P], F32R)

    x_in = sem("x_in")
    ln1_stats, ln1_mv, ln1_ve, ln1_rstd = sem("ln1_stats"), sem("ln1_mv"), sem("ln1_ve"), sem("ln1_rstd")
    h_mid, h_ready, sq_ready, ss_ready = sem("h_mid"), sem("h_ready"), sem("sq_ready"), sem("ss_ready")
    ss_floor, rinv_ready, r_ready, gah_ready, base_ready = (sem(k) for k in (
        "ss_floor", "rinv_ready", "r_ready", "gah_ready", "base_ready"))
    hT_full, hT_ready, rT_full, rT_carry, rT_ready = (sem(k) for k in ("hT_full", "hT_ready", "rT_full", "rT_carry", "rT_ready"))
    v_full, v_ready, kg_full, kg_ready = sem("v_full"), sem("v_ready"), sem("kg_full"), sem("kg_ready")
    gram_full, gram_ready, intra_full, intra_ready, rg_ready = (sem(k) for k in (
        "gram_full", "gram_ready", "intra_full", "intra_ready", "rg_ready"))
    inv0_mid = sem("inv0_mid")
    inv_ready, invT_full, invT_ready = sems("inv_ready", LEVELS), sems("invT_full", LEVELS), sems("invT_ready", LEVELS)
    lv_ready, mi_full, mi_ready, upd_full = (sems(k, LEVELS) for k in ("lv_ready", "mi_full", "mi_ready", "upd_full"))
    pred_full, u_ready, vn_full, vn_ready, ds_full, state_ready = (sems(k, 2) for k in (
        "pred_full", "u_ready", "vn_full", "vn_ready", "ds_full", "state_ready"))
    o_state_ready, oT_ready, ao_full, ao_scaled, x1_ready = sem("o_state_ready"), sem("oT_ready"), sem("ao_full"), sem("ao_scaled"), sem("x1_ready")
    ln2_stats, ln2_mv, ln2_ve, ln2_rstd, xn2_ready = (sem(k) for k in (
        "ln2_stats", "ln2_mv", "ln2_ve", "ln2_rstd", "xn2_ready"))
    h2T_full, h2_ready, xh_ready, xl_ready = sem("h2T_full"), sem("h2_ready"), sem("xh_ready"), sem("xl_ready")
    l_full, l_act, l_ready = sems("l_full", 3), sems("l_act", 3), sems("l_ready", 3)
    prod_ready = sem("prod_ready")
    y_full, y_mid, y_ready = sems("y_full", NB), sems("y_mid", NB), sem("y_ready")
    y_out = sem("y_out")
    low_in, low_used = sem("low_in"), sem("low_used")

    units = [(name, m) for name in ("l1", "l2", "l3") for m in range(HK)] + [("y", 0)]
    chain = [("turn", 0)] + [(name, k) for k in range(1, LEVELS) for name in ("mi", "upd", "turn")]
    chain += [(name, c) for c in range(2) for name in ("pred", "new", "state")] + [("attn_out", 0)]
    mixed = [("start", 0), ("values", 0), ("gram", 0)]
    for k in range(max(len(units), len(chain))):
        mixed += units[k:k + 1] + chain[k:k + 1]
    mixed += [("norm2", 0), ("ln2", 0), ("y", 1)]
    next_norm = {("turn", 2): "stats", ("turn", 3): "norm", ("turn", 4): "unit"}

    def walk(part, has_att, has_mlp, has_next=False, pre=None):
        for name, k in mixed:
            if has_mlp if name in ("l1", "l2", "l3", "y") else has_att:
                part(name, k)
            if has_next and pre and (name, k) in next_norm:
                pre(next_norm[name, k])

    def run(eng, step):
        step(0, 0, 0, True, False, True)
        step(1, 1, 0, True, True, True)
        step(2, 0, 1, True, True, True)
        with eng.Fori(2, STEPS // 2) as i:
            step(2 * i - 1, 1, i - 1, True, True, True)
            step(2 * i, 0, i, True, True, True)
        step(STEPS - 1, 1, STEPS // 2 - 1, True, True, False)
        step(STEPS, 0, STEPS // 2, False, True, False)

    def after(eng, semaphore, value):
        if not isinstance(value, int) or value > 0:
            eng.wait_ge(semaphore, value)

    def tokens(dram, g, t):
        rows = slice(t * P, (t + 1) * P) if isinstance(t, int) else bass.ds(t * P, P)
        return dram[g * NB:(g + 1) * NB, rows, :].rearrange("b p d -> p b d")

    def pairs(ap):
        return ap.rearrange("p (q n) -> p q n", q=NP)

    def nth(n, k):
        return HK * n - (HK - 1 - k)

    blocks = [(q, c, e) for q in range(NP) for c in range(2) for e in range(2)]
    pair_of = [(b, hp) for b in range(NB) for hp in range(H // 2)]

    LOW_UNITS = 3 * HK + 2 * NB
    low_unit = {("l1", m): m for m in range(HK)} | {("l2", m): HK + m for m in range(HK)} | {("l3", m): 2 * HK + m for m in range(HK)}
    low_unit |= {("y", b): 3 * HK + 2 * b for b in range(NB)}

    def low_count(n, u):
        return LOW_UNITS * n - (LOW_UNITS - 1 - u)

    with nc.Block() as block:
        @block.sync
        def _(sp):
            def load_low(n):
                def load(u, parts):
                    if not isinstance(n, int) or n > 1 or u > 0:
                        sp.wait_ge(low_used, low_count(n, u) - 1)
                    for dst, slot, first, count in parts:
                        sp.dma_start(low[:, dst:dst + count, :].bitcast(F32), low_dram[slot].rearrange("p (b n) -> p b n", n=P)[:, first:first + count, :]).then_inc(low_in, 32 // len(parts))

                for m in range(HK):
                    load(m, [(KT * i, (w + KT * m) // SLOT, (w + KT * m) % SLOT, KT) for i, w in enumerate((BLK_W1, BLK_W2))])
                for i, w in enumerate((BLK_H1, BLK_H2)):
                    for m in range(HK):
                        load(HK * (i + 1) + m, [(0, (w + HK * m) // SLOT, 0, SLOT)])
                for b in range(NB):
                    for i in range(2):
                        load(low_unit["y", b] + i, [(0, BLK_W3 // SLOT + i, 0, SLOT)])

            def program(general):
                run(sp, lambda *args: step(general, *args))

            def step(general, n, g, t, has_att, has_mlp, has_next):
                if has_next:
                    sp.wait_ge(base_ready, n + 1)
                    sp.dma_start(xin[:], tokens(x, 1 - g, t + g)).then_inc(x_in, 16)
                if has_mlp and general:
                    load_low(n)
                if has_mlp:
                    sp.wait_ge(y_ready, n)
                    sp.dma_start(tokens(out, 1 - g, t + g - 1), y[:]).then_inc(y_out, 16)

            sp.dma_start(xin[:], tokens(x, 0, 0)).then_inc(x_in, 16)
            any_low = sp.value_load(flag_i[0:1, 0:1], min_val=0, max_val=1)
            with sp.If(any_low > 0):
                program(True)
            with sp.Else():
                program(False)
            sp.wait_ge(y_out, 16 * STEPS)

        @block.gpsimd
        def _(pool):
            def rsqrt(dst, src, done):
                pool.tensor_tensor(dst[:], src[:], minus_half[:, 0:src.shape[1]], ALU.pow).then_inc(done, 1)

            def pre(name, nxt):
                if name == "stats":
                    pool.wait_ge(ln1_ve, nxt)
                    rsqrt(rstd1, ve1, ln1_rstd)
                if name == "norm":
                    pool.wait_ge(ss_floor, nxt)
                    rsqrt(rinv, ssm, rinv_ready)

            def residual(g, nxt, now):
                pool.wait_ge(h_ready, nxt)
                pool.tensor_tensor(gah[:], h[:], ga[:, g * NB:(g + 1) * NB, :], ALU.mult).then_inc(gah_ready, 1)
                pool.wait_ge(gah_ready, nxt)
                if now is not None:
                    pool.wait_ge(x1_ready, now)
                pool.tensor_tensor(base[:], xin[:], gah[:], ALU.add).then_inc(base_ready, 1)

            def step(n, g, t, has_att, has_mlp, has_next):
                now = n + 1

                def part(name, k):
                    if name == "start":
                        pool.wait_ge(rT_ready, now)
                        pool.tensor_tensor(rg[:].rearrange("p (b q) n -> p b q n", b=NB),
                                           rT[g][:, :, 1:P + 1].rearrange("p (b q) n -> p b q n", b=NB),
                                           head_decay[:].rearrange("p q c n -> p q (c n)").unsqueeze(1).to_broadcast([P, NB, H // 2, P]),
                                           ALU.mult).then_inc(rg_ready, 1)
                    if name == "gram" or (name == "mi" and k < LEVELS - 1):
                        level = k + 1
                        if level == 1:
                            pool.wait_ge(gram_ready, now)
                        if level >= 3:
                            pool.wait_ge(mi_full[level - 2], now)
                        pool.tensor_tensor(lv[level % 2][:].rearrange("p (b q) c n -> p b (q c n)", b=NB),
                                           gram[:].rearrange("p (b q) c n -> p b (q c n)", b=NB),
                                           level_mask[:, level].rearrange("p q c n -> p (q c n)").unsqueeze(1).to_broadcast([P, NB, 2 * P]),
                                           ALU.mult).then_inc(lv_ready[level], 1)
                    if name == "attn_out":
                        pool.wait_ge(ln2_ve, now)
                        rsqrt(rstd2, ve2, ln2_rstd)
                        if has_next:
                            residual(1 - g, n + 2, now)

                walk(part, has_att, has_mlp, has_next, lambda name: pre(name, n + 2))

            pre("stats", 1)
            pre("norm", 1)
            residual(0, 1, None)
            run(pool, step)

        @block.scalar
        def _(act):
            def step(n, g, t, has_att, has_mlp, has_next):
                now = n + 1

                def part(name, k):
                    if name == "start":
                        act.wait_ge(hT_full, now)
                        act.copy(hT[:].rearrange("p k b n -> p (k b n)"), duo[0][:, 0, :]).then_inc(hT_ready, 1)
                    if name == "values":
                        act.wait_ge(v_full, now)
                        act.copy(v[:].rearrange("p b n -> p (b n)"), solo[0][:]).then_inc(v_ready, 1)
                    if name == "gram":
                        act.wait_ge(gram_full, now)
                        act.copy(gram[:].rearrange("p q c n -> p (q c n)"), duo[0][:, 0, :]).then_inc(gram_ready, 1)
                    if name == "turn":
                        act.wait_ge(invT_full[k], now)
                        act.copy(invT[:].rearrange("p q e n -> p (q e n)"), solo[0][:]).then_inc(invT_ready[k], 1)
                    if name == "mi":
                        act.wait_ge(mi_full[k], now)
                        act.copy(mi[:].rearrange("p e q n -> p e (q n)"), duo[1][:, :, 0:NP * C]).then_inc(mi_ready[k], 1)
                    if name == "new":
                        act.wait_ge(vn_full[k], now)
                        act.copy(vn[half(k)].rearrange("p q e n -> p (q e n)"), solo[1][half(k), :]).then_inc(vn_ready[k], 1)
                    if name == "state" and k == 1:
                        act.wait_ge(ds_full[1], now)
                        act.copy(o_state[:].rearrange("p q n -> p (q n)"), duo[0][:, 1, :]).then_inc(o_state_ready, 1)
                    if name == "ln2":
                        act.wait_ge(h2T_full, now)
                        for kt in range(KT):
                            for b in range(NB):
                                ins = act.activation(h2[:, kt, b, :], solo[1][:, (kt * NB + b) * P:(kt * NB + b + 1) * P], ACT.Identity,
                                                     bias=sbm[:, kt, g * NB + b:g * NB + b + 1],
                                                     scale=cb1[:, kt, g * NB + b:g * NB + b + 1])
                        ins.then_inc(h2_ready, 1)
                    if name == "l1":
                        act.wait_ge(l_full[0], nth(n, k))
                        if k >= 2:
                            act.wait_ge(prod_ready, nth(n, k - 2))
                        act.activation(gate[k % 2][:], mlp[k % 2][:, 0:TOK], ACT.Silu,
                                       scale=scale_sb[:, 0, k:k + 1]).then_inc(l_act[0], 1)
                    if name in ("l2", "l3"):
                        layer = 1 if name == "l2" else 2
                        act.wait_ge(l_full[layer], nth(n, k))
                        if k >= 2:
                            act.wait_ge(l_ready[layer], nth(n, k - 2))
                        else:
                            act.wait_ge(l_ready[layer - 1], nth(n, HK - 2 + k))
                        s = scale_sb[:, layer + 1, k:k + 1]
                        act.activation(full[k % 2][:], mlp[k % 2][:, 0:TOK], ACT.Gelu, scale=s)
                        act.activation(act_hi[layer % 2][:, k, :], mlp[k % 2][:, 0:TOK], ACT.Gelu, scale=s).then_inc(l_act[layer], 1)

                walk(part, has_att, has_mlp)

            run(act, step)

        @block.vector
        def _(dve):
            def norm_stats(src, st, mv, ve, count, stats_done, mv_done, ve_done):
                for b in range(NB):
                    ins = dve.bn_stats(st[:, b, :], src[:, b, :])
                ins.then_inc(stats_done, 1)
                dve.wait_ge(flag_set, 1)
                dve.wait_ge(stats_done, count)
                for b in range(NB):
                    ins = dve.bn_aggr(mv[:, b, :], st[:, b, :])
                ins.then_inc(mv_done, 1)
                dve.wait_ge(mv_done, count)
                dve.tensor_scalar(ve[:], mv[:, :, 1], EPS, None, ALU.add).then_inc(ve_done, 1)

            def pre(name, g, nxt):
                if name == "stats":
                    dve.wait_ge(x_in, 16 * nxt)
                    norm_stats(xin, st1, mv1, ve1, nxt, ln1_stats, ln1_mv, ln1_ve)
                if name == "norm":
                    dve.wait_ge(ln1_rstd, nxt)
                    after(dve, base_ready, nxt - 1)
                    for b in range(NB):
                        ins = dve.scalar_tensor_tensor(h[:, b, :], xin[:, b, :], mv1[:, b, 0:1], ca1[:, g * NB + b, :], ALU.subtract, ALU.mult)
                    ins.then_inc(h_mid, 1)
                    dve.wait_ge(h_mid, nxt)
                    for b in range(NB):
                        ins = dve.scalar_tensor_tensor(h[:, b, :], h[:, b, :], rstd1[:, b:b + 1], sa[:, g * NB + b, :], ALU.mult, ALU.add)
                    ins.then_inc(h_ready, 1)
                    dve.wait_ge(h_ready, nxt)
                    dve.tensor_tensor(r[:], h[:], h[:], ALU.mult).then_inc(sq_ready, 1)
                    dve.wait_ge(sq_ready, nxt)
                    dve.tensor_reduce(ss[:], r[:].rearrange("p b (h d) -> p (b h) d", h=H), AX.X, ALU.add).then_inc(ss_ready, 1)
                    dve.wait_ge(ss_ready, nxt)
                    dve.tensor_scalar(ssm[:], ss[:], 1e-24, None, ALU.max).then_inc(ss_floor, 1)
                if name == "unit":
                    dve.wait_ge(rinv_ready, nxt)
                    dve.tensor_tensor(r[:].rearrange("p b (h d) -> p (b h) d", h=H), h[:].rearrange("p b (h d) -> p (b h) d", h=H),
                                      rinv[:].unsqueeze(2).to_broadcast([P, NB * H, DH]), ALU.mult).then_inc(r_ready, 1)

            def step(n, g, t, has_att, has_mlp, has_next):
                now = n + 1

                def part(name, k):
                    if name == "start":
                        dve.wait_ge(rT_full, now)
                        dve.tensor_copy(rT[g][:, :, 0:1], rT[g][:, :, P:P + 1]).then_inc(rT_carry, 1)
                        dve.wait_ge(rT_carry, now)
                        dve.tensor_copy(rT[g][:, :, 1:P + 1], pairs(duo[0][:, 1, :])).then_inc(rT_ready, 1)
                    if name == "values":
                        dve.wait_ge(kg_full, now)
                        dve.tensor_tensor(kg[:].rearrange("p (b q) e d -> p b (q e) d", b=NB),
                                          solo[1][:].rearrange("p (b h d) -> p b h d", b=NB, h=H),
                                          tail_decay[:].unsqueeze(1).unsqueeze(3).to_broadcast([P, NB, H, DH]), ALU.mult).then_inc(kg_ready, 1)
                    if name == "gram":
                        dve.wait_ge(gram_ready, now)
                        dve.tensor_tensor(inv[:].rearrange("p (b q) c n -> p b (q c n)", b=NB),
                                          gram[:].rearrange("p (b q) c n -> p b (q c n)", b=NB),
                                          level_mask[:, 0].rearrange("p q c n -> p (q c n)").unsqueeze(1).to_broadcast([P, NB, 2 * P]),
                                          ALU.mult).then_inc(inv0_mid, 1)
                        dve.wait_ge(intra_full, now)
                        dve.tensor_tensor(intra[:].rearrange("p e (b q) n -> p e b (q n)", b=NB),
                                          duo[1][:, :, 0:NP * C].rearrange("p e (b n) -> p e b n", b=NB),
                                          intra_mask[:].rearrange("p e q n -> p e (q n)").unsqueeze(2).to_broadcast([P, 2, NB, P]),
                                          ALU.mult).then_inc(intra_ready, 1)
                        dve.wait_ge(inv0_mid, now)
                        dve.tensor_tensor(inv[:].rearrange("p q c n -> p (q c) n"), inv[:].rearrange("p q c n -> p (q c) n"),
                                          con[:, CO_EYE:CO_EYE + C].unsqueeze(1).to_broadcast([P, 2 * NP, C]), ALU.add).then_inc(inv_ready[0], 1)
                    if name == "upd":
                        dve.wait_ge(upd_full[k], now)
                        by_chunk = inv[:].rearrange("p q c n -> p c q n")
                        dve.tensor_tensor(by_chunk, by_chunk, duo[0][:, :, 0:NP * C].rearrange("p c (q n) -> p c q n", q=NP), ALU.subtract).then_inc(inv_ready[k], 1)
                    if name == "pred":
                        if k == 0:
                            dve.wait_ge(v_ready, now)
                        dve.wait_ge(pred_full[k], now)
                        by_head = v[half(k)].rearrange("p b (q e d) -> p e (b q) d", e=2, d=DH)
                        dve.tensor_tensor(by_head, by_head, duo[1][half(k), :, 0:NP * DH].rearrange("p e (q d) -> p e q d", q=NP), ALU.subtract).then_inc(u_ready[k], 1)
                    if name == "state":
                        dve.wait_ge(ds_full[k], now)
                        s = state[g][:].rearrange("p (b q) d -> p q b d", b=NB)
                        ds = solo[0][:, 0:NP * DH].rearrange("p (b q d) -> p q b d", b=NB, d=DH)
                        for q in range(H // 2):
                            ins = dve.scalar_tensor_tensor(s[:, q], s[:, q], chunk_decay[:, q:q + 1], ds[:, q], ALU.mult, ALU.add)
                        ins.then_inc(state_ready[k], 1)
                        if k == 1:
                            dve.wait_ge(o_state_ready, now)
                            dve.tensor_tensor(oT[:].rearrange("p q n -> p (q n)"), o_state[:].rearrange("p q n -> p (q n)"),
                                              duo[0][:, 0, :], ALU.add).then_inc(oT_ready, 1)
                    if name == "attn_out":
                        xo = x1[g]
                        dve.wait_ge(ao_full, now)
                        dve.tensor_tensor(xo[:], duo[1][:, 0, :].rearrange("p (b n) -> p b n", b=NB),
                                          ga[:, g * NB:(g + 1) * NB, :], ALU.mult).then_inc(ao_scaled, 1)
                        dve.wait_ge(ao_scaled, now)
                        dve.wait_ge(base_ready, now)
                        dve.tensor_tensor(xo[:], xo[:], base[:], ALU.add).then_inc(x1_ready, 1)
                        dve.wait_ge(x1_ready, now)
                        norm_stats(xo, st2, mv2, ve2, now, ln2_stats, ln2_mv, ln2_ve)
                    if name == "norm2":
                        dve.wait_ge(ln2_rstd, now)
                        for b in range(NB):
                            ins = dve.tensor_scalar(xn2[:, b, :], x1[g][:, b, :], mv2[:, b, 0:1], rstd2[:, b:b + 1], ALU.subtract, ALU.mult)
                        ins.then_inc(xn2_ready, 1)
                    if name == "ln2":
                        dve.wait_ge(h2_ready, now)
                        flat = h2[:].rearrange("p k b n -> p k (b n)")
                        dve.tensor_copy(xh[:], flat).then_inc(xh_ready, 1)
                        dve.wait_ge(xh_ready, now)
                        dve.tensor_tensor(xl[:], flat, xh[:].bitcast(F32), ALU.subtract).then_inc(xl_ready, 1)
                    if name == "l1":
                        dve.wait_ge(l_act[0], nth(n, k))
                        up, s = mlp[k % 2][:, TOK:2 * TOK], scale_sb[:, 1, k:k + 1]
                        dve.scalar_tensor_tensor(full[k % 2][:], up, s, gate[k % 2][:], ALU.mult, ALU.mult)
                        dve.scalar_tensor_tensor(act_hi[0][:, k, :], up, s, gate[k % 2][:], ALU.mult, ALU.mult).then_inc(prod_ready, 1)
                        dve.wait_ge(prod_ready, nth(n, k))
                    if name in ("l2", "l3"):
                        dve.wait_ge(l_act[1 if name == "l2" else 2], nth(n, k))
                    if name in ("l1", "l2", "l3"):
                        layer = ("l1", "l2", "l3").index(name)
                        dve.tensor_tensor(act_lo[layer % 2][:, k, :], full[k % 2][:], act_hi[layer % 2][:, k, :].bitcast(F32),
                                          ALU.subtract).then_inc(l_ready[layer], 1)
                    if name == "y":
                        dve.wait_ge(y_full[k], n)
                        if k == 0:
                            after(dve, y_out, 16 * (n - 1))
                        dve.tensor_tensor(y[:, k, :], mlp[k][:, 0:D], gbs[:, (1 - g) * NB + k, :], ALU.mult).then_inc(y_mid[k], 1)
                        dve.wait_ge(y_mid[k], n)
                        ins = dve.tensor_tensor(y[:, k, :], y[:, k, :], x1[1 - g][:, k, :], ALU.add)
                        if k == NB - 1:
                            ins.then_inc(y_ready, 1)

                walk(part, has_att, has_mlp, has_next, lambda name: pre(name, 1 - g, n + 2))

            for name in ("stats", "norm", "unit"):
                pre(name, 0, 1)
            run(dve, step)

        @block.tensor
        def _(pe):
            def program(general):
                run(pe, lambda *args: step(general, *args))

            def step(general, n, g, t, has_att, has_mlp, has_next):
                now = n + 1

                def low_ready(u):
                    pe.wait_ge(low_in, 32 * low_count(n, u))

                def layer(name, k):
                    bank = mlp[k % 2]
                    if name == "l1":
                        if k == 0:
                            pe.wait_ge(xl_ready, n)
                        if k == 1:
                            after(pe, y_ready, n - 1)
                        if k >= 2:
                            pe.wait_ge(l_ready[0], nth(n, k - 2))
                        if general:
                            low_ready(low_unit[name, k])
                        for i, w in enumerate((BLK_W1, BLK_W2)):
                            dst = bank[:, i * TOK:(i + 1) * TOK]
                            for j in range(KT):
                                pe.matmul(dst, w_hi[:, w + KT * k + j, :], xh[:, j, :], start=j == 0, stop=False)
                                if general:
                                    for x_part in (xh, xl):
                                        mm = pe.matmul(dst, low[:, KT * i + j, :], x_part[:, j, :], start=False, stop=False)
                                        if i == 1 and j == KT - 1 and x_part is xl:
                                            mm.then_inc(low_used, 1)
                                mm = pe.matmul(dst, w_hi[:, w + KT * k + j, :], xl[:, j, :], start=False, stop=j == KT - 1)
                        mm.then_inc(l_full[0], 1)
                    if name in ("l2", "l3"):
                        i = 1 if name == "l2" else 2
                        hi, lo = act_hi[(i - 1) % 2], act_lo[(i - 1) % 2]
                        dst = bank[:, 0:TOK]
                        w = (BLK_H1 if i == 1 else BLK_H2) + HK * k
                        if k == 0:
                            pe.wait_ge(l_ready[i - 1], nth(n, HK - 2))
                        if k == 1:
                            pe.wait_ge(l_ready[i - 1], nth(n, HK - 1))
                        if k >= 2:
                            pe.wait_ge(l_act[i], nth(n, k - 2))
                        if general:
                            low_ready(low_unit[name, k])
                        for j in range(HK):
                            if k == 0:
                                pe.wait_ge(l_ready[i - 1], nth(n, j))
                            pe.matmul(dst, w_hi[:, w + j, :], hi[:, j, :], start=j == 0, stop=False)
                            if general:
                                pe.matmul(dst, low[:, j, :], hi[:, j, :], start=False, stop=False)
                                mm = pe.matmul(dst, low[:, j, :], lo[:, j, :], start=False, stop=False)
                                if j == HK - 1:
                                    mm.then_inc(low_used, 1)
                            mm = pe.matmul(dst, w_hi[:, w + j, :], lo[:, j, :], start=False, stop=j == HK - 1)
                        mm.then_inc(l_full[i], 1)
                    if name == "y":
                        hi, lo = act_hi[0], act_lo[0]
                        rows = slice(k * P, (k + 1) * P)
                        if k == 0:
                            pe.wait_ge(l_ready[2], nth(n, HK - 2))
                        for j in range(HK):
                            if k == 0:
                                pe.wait_ge(l_ready[2], nth(n, j))
                            w3 = w_hi[:, BLK_W3 + KT * j:BLK_W3 + KT * (j + 1), :].rearrange("p a n -> p (a n)")
                            pe.matmul(bank[:, 0:D], hi[:, j, rows], w3, start=j == 0, stop=False)
                            if general:
                                u = low_unit[name, k] + j // (HK // 2)
                                if j % (HK // 2) == 0:
                                    low_ready(u)
                                first = KT * (j % (HK // 2))
                                w3_low = low[:, first:first + KT, :].rearrange("p a n -> p (a n)")
                                pe.matmul(bank[:, 0:D], hi[:, j, rows], w3_low, start=False, stop=False)
                                mm = pe.matmul(bank[:, 0:D], lo[:, j, rows], w3_low, start=False, stop=False)
                                if j % (HK // 2) == HK // 2 - 1:
                                    mm.then_inc(low_used, 1)
                            mm = pe.matmul(bank[:, 0:D], lo[:, j, rows], w3, start=False, stop=j == HK - 1)
                        mm.then_inc(y_full[k], 1)

                def part(name, k):
                    if name in ("l1", "l2", "l3", "y"):
                        layer(name, k)
                    if name == "start":
                        pe.wait_ge(h_ready, now)
                        for kt in range(KT):
                            for b in range(NB):
                                mm = pe.transpose(duo[0][:, 0, (kt * NB + b) * P:(kt * NB + b + 1) * P], h[:, b, kt * P:(kt + 1) * P], ident)
                        mm.then_inc(hT_full, 1)
                        pe.wait_ge(r_ready, now)
                        for q, (b, hp) in enumerate(pair_of):
                            mm = pe.transpose(duo[0][:, 1, q * P:(q + 1) * P], r[:, b, hp * P:(hp + 1) * P], ident)
                        mm.then_inc(rT_full, 1)
                    if name == "values":
                        pe.wait_ge(rT_ready, now)
                        after(pe, h2_ready, n)
                        for q in range(NP):
                            mm = pe.transpose(solo[1][:, q * P:(q + 1) * P], rT[g][:, q, 0:P], ident)
                        mm.then_inc(kg_full, 1)
                        pe.wait_ge(hT_ready, now)
                        for b in range(NB):
                            for kt in range(KT):
                                mm = pe.matmul(solo[0][:, b * D:(b + 1) * D], hT[:, kt, b, :], wv_sb[:, kt, :], start=kt == 0, stop=kt == KT - 1)
                        mm.then_inc(v_full, 1)
                    if name == "gram":
                        for q, c, e in blocks:
                            keys = rT[g][half(e), q, C * c:C * c + C]
                            mm = pe.matmul(duo[0][half(e), 0, q * P + C * c:q * P + C * c + C], keys, keys, start=True, stop=True)
                        mm.then_inc(gram_full, 1)
                        for q, c, e in blocks:
                            mm = pe.matmul(duo[1][half(c), e, q * C:(q + 1) * C], rT[g][half(e), q, C * c:C * c + C],
                                           rT[g][half(e), q, C * c + 1:C * c + C + 1], start=True, stop=True)
                        mm.then_inc(intra_full, 1)
                    if name == "turn":
                        if k == 0:
                            pe.wait_ge(v_ready, now)
                        pe.wait_ge(inv_ready[k], now)
                        for q in range(NP):
                            mm = pe.transpose(solo[0][:, q * P:(q + 1) * P], inv[:, q].rearrange("p c n -> p (c n)"), ident)
                        mm.then_inc(invT_full[k], 1)
                    if name == "mi":
                        pe.wait_ge(flag_row, 1)
                        if k == 1:
                            pe.wait_ge(kg_ready, now)
                        pe.wait_ge(lv_ready[k], now)
                        for q, c, e in blocks:
                            mm = pe.matmul(duo[1][half(c), e, q * C:(q + 1) * C], lv[k % 2][half(e), q, c, :],
                                           inv[half(e), q, c, :], start=True, stop=True)
                        mm.then_inc(mi_full[k], 1)
                    if name == "upd":
                        pe.wait_ge(flag_row, 1)
                        pe.wait_ge(invT_ready[k - 1], now)
                        pe.wait_ge(mi_ready[k], now)
                        for q, c, e in blocks:
                            mm = pe.matmul(duo[0][half(e), c, q * C:(q + 1) * C], invT[half(c), q, e, :],
                                           mi[half(c), e, q, :], start=True, stop=True)
                        mm.then_inc(upd_full[k], 1)
                    if name == "pred":
                        pe.wait_ge(flag_row, 1)
                        if k == 0:
                            pe.wait_ge(intra_ready, now)
                        else:
                            pe.wait_ge(state_ready[0], now)
                        for q in range(NP):
                            for e in range(2):
                                mm = pe.matmul(duo[1][half(k), e, q * DH:(q + 1) * DH], rT[g][half(e), q, C * k:C * k + C],
                                               state[g][half(e), q, :], start=True, stop=True)
                        mm.then_inc(pred_full[k], 1)
                    if name == "new":
                        pe.wait_ge(flag_row, 1)
                        if k == 0:
                            pe.wait_ge(invT_ready[LEVELS - 1], now)
                        pe.wait_ge(u_ready[k], now)
                        for q, (b, hp) in enumerate(pair_of):
                            for e in range(2):
                                hd = hp * 2 + e
                                mm = pe.matmul(solo[1][half(k), q * P + DH * e:q * P + DH * e + DH], invT[half(k), q, e, :],
                                               v[half(k), b, hd * DH:(hd + 1) * DH], start=True, stop=True)
                        mm.then_inc(vn_full[k], 1)
                    if name == "state":
                        pe.wait_ge(flag_row, 1)
                        if k == 0:
                            pe.wait_ge(rg_ready, now)
                        pe.wait_ge(vn_ready[k], now)
                        for q in range(NP):
                            for e in range(2):
                                cols = slice(q * P + C * k, q * P + C * k + C)
                                pe.matmul(duo[0][half(e), 1, cols], state[g][half(e), q, :], rg[half(e), q, C * k:C * k + C], start=True, stop=True)
                                pe.matmul(duo[0][half(e), 0, cols], vn[half(k), q, e, :], intra[half(k), e, q, :], start=True, stop=True)
                                mm = pe.matmul(solo[0][half(e), q * DH:(q + 1) * DH], kg[half(k), q, e, :], vn[half(k), q, e, :], start=True, stop=True)
                        mm.then_inc(ds_full[k], 1)
                    if name == "attn_out":
                        pe.wait_ge(oT_ready, now)
                        for b in range(NB):
                            for hp in range(H // 2):
                                mm = pe.matmul(duo[1][:, 0, b * D:(b + 1) * D], oT[:, b * (H // 2) + hp, :], wr_sb[:, hp, :],
                                               start=hp == 0, stop=hp == H // 2 - 1)
                        mm.then_inc(ao_full, 1)
                    if name == "ln2":
                        pe.wait_ge(xn2_ready, now)
                        for kt in range(KT):
                            for b in range(NB):
                                mm = pe.transpose(solo[1][:, (kt * NB + b) * P:(kt * NB + b + 1) * P], xn2[:, b, kt * P:(kt + 1) * P], ident)
                        mm.then_inc(h2T_full, 1)

                walk(part, has_att, has_mlp)

            any_low = pe.value_load(flag_i[0:1, 0:1], min_val=0, max_val=1)
            with pe.If(any_low > 0):
                program(True)
            with pe.Else():
                program(False)


INPUTS = ("x", "wts", "wv", "wr", "wmod", "cT", "cB", "scales", "s3", "dec_pair", "dec_all", "alpha_pair", "const")


def kernel(**inputs):
    import concourse.bacc as bacc
    from concourse.bass_utils import run_bass_kernel_spmd

    a = {k[3:]: np.asarray(v) for k, v in inputs.items()}

    def turned(w):
        o, i = w.shape
        return w.reshape(o // P, P, i // P, P).transpose(3, 0, 2, 1).reshape(P, -1, P)

    w3 = a["ffn_w3_w"].reshape(KT, P, HK, P).transpose(3, 2, 0, 1).reshape(P, -1, P)
    blocks = np.concatenate([turned(a["ffn_w1_w"]), turned(a["ffn_w2_w"]), turned(a["ffn_h1_w"]), turned(a["ffn_h2_w"]), w3], 1)
    rows = lambda w: w.reshape(KT, P, -1).transpose(1, 0, 2)
    cT = rows(a["c"].T)
    pair = lambda z: np.repeat(z.reshape(H // 2, 2).T, C, axis=0)
    arrays = {
        "x": a["attn_out"],
        "wts": blocks.reshape(P, SLOTS, SLOT * P).transpose(1, 0, 2),
        "wv": rows(a["attn_Ww"].T),
        "wr": rows(a["attn_Wr"].T),
        "wmod": rows(a["wmod"]),
        "cT": cT,
        "cB": np.repeat(cT[:, :, :, None], P, axis=3),
        "scales": np.stack([a["ffn_" + k].reshape(HK, P).T for k in ("w1_s", "w2_s", "h1_s", "h2_s")], 1),
        "s3": np.repeat(a["ffn_w3_s"][None], P, axis=0),
        "dec_pair": pair(a["attn_decay"]),
        "dec_all": np.repeat(a["attn_decay"][None], P, axis=0),
        "alpha_pair": pair(a["attn_log_alpha"]),
        "const": constants(),
    }
    arrays = {k: np.ascontiguousarray(v) for k, v in arrays.items()}
    nc = bacc.Bacc("TRN2", target_bir_lowering=False, num_devices=1, dynamic_dma_scratch_size=1024)
    aps = [nc.dram_tensor(f"in_{k}", arrays[k].shape, F32, kind="ExternalInput").ap() for k in INPUTS]
    out = nc.dram_tensor("out_y", (B, T, D), F32, kind="ExternalOutput").ap()
    adaln_block(nc, *aps, out)
    r = run_bass_kernel_spmd(nc, [{f"in_{k}": arrays[k] for k in INPUTS}], core_ids=[0])
    return r.results[0]["out_y"]
```

```python
from contextlib import ExitStack

import numpy as np

import concourse.bass as bass
from concourse import mybir

F32 = mybir.dt.float32
F32R = mybir.dt.float32r
I32 = mybir.dt.int32
ACT = mybir.ActivationFunctionType
ALU = mybir.AluOpType
AX = mybir.AxisListType

P = 128
B, T, D = 4, 2048, 256
H, DH, C = 4, 64, 64
HID = 1024
KT = D // P
HK = HID // P
NB = 2
NG = B // NB
NP = NB * (H // 2)
STEPS = (T // P) * NG
TOK = NB * P
LEVELS = 6
HB = C // 2
EPS = 1e-5

BLK_W1, BLK_W2 = 0, HK * KT
BLK_H1 = BLK_W2 + HK * KT
BLK_H2 = BLK_H1 + HK * HK
BLK_W3 = BLK_H2 + HK * HK
BLOCKS = BLK_W3 + HK * KT
SLOT = 8
SLOTS = BLOCKS // SLOT
STAGES = 4

CO_ID, CO_EYE = 0, P
CO_MASK = CO_EYE + HB
CO_UP = CO_MASK + LEVELS * C
CO_DIST = CO_UP + C
CO_ROW0 = CO_DIST + C
CO_BLK = CO_ROW0 + P
CO_E = CO_BLK + 2
CO_N = CO_E + 1


def constants():
    c = np.zeros((P, CO_N), np.float32)
    p = np.arange(P)[:, None]
    j, i = p % C, np.arange(C)[None, :]
    c[:, CO_ID:CO_ID + P] = np.eye(P)
    c[:, CO_EYE:CO_EYE + HB] = j % HB == np.arange(HB)[None, :]
    c[:, CO_MASK:CO_MASK + C] = -1.0 * ((j >> 1 == i >> 1) & (j > i))
    for k in range(1, LEVELS - 1):
        c[:, CO_MASK + k * C:CO_MASK + (k + 1) * C] = (
            (j >> (k + 1) == i >> (k + 1)) & ((i >> k) % 2 == 1) & ((j >> k) % 2 == 0))
    k = LEVELS - 1
    c[:, CO_MASK + k * C:CO_MASK + (k + 1) * C] = (j >= HB) & (i < HB)
    c[:, CO_UP:CO_UP + C] = i > j
    c[:, CO_DIST:CO_DIST + C] = np.abs(i - j)
    c[0, CO_ROW0:CO_ROW0 + P] = 1.0
    for k in range(2):
        c[:, CO_BLK + k] = j[:, 0] // HB == k
    c[:, CO_E] = np.e
    return c


def half(k):
    return slice(C * k, C * k + C)


def adaln_block(nc, x, wts, wv, wr, wmod, cT, cB, scales, s3, dec_pair, dec_all, alpha_pair, const, out):
    with ExitStack() as ctx:
        def sb(name, shape, dt=F32, c=ctx):
            return c.enter_context(nc.sbuf_tensor(name, [P] + list(shape), dt))

        def sem(name):
            return ctx.enter_context(nc.semaphore(name))

        def sems(name, n):
            return [sem(f"{name}{i}") for i in range(n)]

        duo = [ctx.enter_context(nc.psum_tensor(f"duo{i}", [P, 2, 512], F32)) for i in range(2)]
        solo = [ctx.enter_context(nc.psum_tensor(f"solo{i}", [P, 512], F32)) for i in range(2)]
        mlp = [ctx.enter_context(nc.psum_tensor(f"mlp{i}", [P, 512], F32)) for i in range(2)]

        w_hi = sb("w_hi", [BLOCKS, P], F32R)
        wv_sb = sb("wv_sb", [KT, D])
        wr_sb = sb("wr_sb", [KT, D])
        con = sb("con", [CO_N])
        scale_sb = sb("scale_sb", [4, HK])
        ca1 = sb("ca1", [B, D])
        sa = sb("sa", [B, D])
        ga = sb("ga", [B, D])
        gbs = sb("gbs", [B, D])
        cb1 = sb("cb1", [KT, B])
        sbm = sb("sbm", [KT, B])
        level_mask = sb("level_mask", [LEVELS, 2, H // 2, C])
        intra_mask = sb("intra_mask", [2, NB, H // 2, C])
        head_decay = sb("head_decay", [H // 2, 2, C])
        tail_decay = sb("tail_decay", [H])
        chunk_decay = sb("chunk_decay", [H // 2])
        minus_half = sb("minus_half", [NB * H])
        flag_i = sb("flag_i", [1], I32)
        slot_max = sb("slot_max", [SLOTS])
        state = [sb(f"state{g}", [NP, DH]) for g in range(NG)]
        rT = [sb(f"rT{g}", [NP, P + 1]) for g in range(NG)]
        with ExitStack() as early:
            wst = [sb(f"wst{s}", [SLOT * P], F32, early) for s in range(STAGES)]
            lost = [sb(f"lost{s}", [SLOT * P], F32, early) for s in range(STAGES)]
        act_hi = [sb(f"act_hi{i}", [HK, TOK], F32R) for i in range(2)]
        act_lo = [sb(f"act_lo{i}", [HK, TOK], F32R) for i in range(2)]

        const_in, c_in, small_in, wst_in = sem("const_in"), sem("c_in"), sem("small_in"), sems("wst_in", STAGES)
        hi_done, lo_done, max_done = sem("hi_done"), sem("lo_done"), sem("max_done")
        flag_col, flag_row, flag_max, flag_set = sem("flag_col"), sem("flag_row"), sem("flag_max"), sem("flag_set")
        pool_set, dve_set, act_set, pe_set = sem("pool_set"), sem("dve_set"), sem("act_set"), sem("pe_set")

        with ExitStack() as tmp:
            wmod_sb = sb("wmod_sb", [KT, 6 * D], F32, tmp)
            cT_sb = sb("cT_sb", [KT, B], F32, tmp)
            cB_sb = sb("cB_sb", [KT, B, P], F32, tmp)
            scT = sb("scT", [KT, B], F32, tmp)
            scB = sb("scB", [KT, B, P], F32, tmp)
            s3_sb = sb("s3_sb", [D], F32, tmp)
            dec = sb("dec", [H // 2 + H + H // 2], F32, tmp)
            gam = sb("gam", [H // 2 + H + H // 2], F32, tmp)
            edec = sb("edec", [H // 2 + H + H // 2], F32, tmp)
            dist_pow = sb("dist_pow", [2, H // 2, C], F32, tmp)
            sgn = sb("sgn", [2, B, D], F32, tmp)
            mag = sb("mag", [2, B, D], F32, tmp)
            NPAIR = H // 2
            DEC_PAIR, DEC_ALL, DEC_ALPHA = slice(0, NPAIR), slice(NPAIR, NPAIR + H), slice(NPAIR + H, NPAIR + H + NPAIR)

            with nc.Block() as block:
                @block.sync
                def _(sp):
                    sp.dma_start(con[:], const).then_inc(const_in, 16)
                    sp.dma_start(dec[:, DEC_PAIR], dec_pair).then_inc(const_in, 16)
                    sp.dma_start(dec[:, DEC_ALL], dec_all).then_inc(const_in, 16)
                    sp.dma_start(dec[:, DEC_ALPHA], alpha_pair).then_inc(const_in, 16)
                    for s in range(STAGES):
                        sp.dma_start(wst[s][:], wts[s]).then_inc(wst_in[s], 16)

                @block.scalar
                def _(act):
                    for dst, src in ((cT_sb, cT), (cB_sb, cB), (wmod_sb, wmod)):
                        act.dma_start(dst[:], src).then_inc(c_in, 16)
                    for dst, src in ((s3_sb, s3), (scale_sb, scales), (wv_sb, wv), (wr_sb, wr)):
                        act.dma_start(dst[:], src).then_inc(small_in, 16)
                    act.wait_ge(c_in, 3 * 16)
                    act.activation(scT[:], cT_sb[:], ACT.Silu).then_inc(act_set, 1)
                    act.activation(scB[:], cB_sb[:], ACT.Silu).then_inc(act_set, 1)

                @block.gpsimd
                def _(pool):
                    pool.memset(minus_half[:], -0.5).then_inc(pool_set, 1)
                    for g in range(NG):
                        pool.memset(state[g][:], 0.0)
                        pool.memset(rT[g][:], 0.0).then_inc(pool_set, 1)
                    pool.wait_ge(const_in, 64)
                    pool.tensor_scalar(edec[:, 0:NPAIR + H], dec[:, 0:NPAIR + H], -1.0, None, ALU.mult).then_inc(pool_set, 1)
                    pool.tensor_copy(edec[:, DEC_ALPHA], dec[:, DEC_ALPHA]).then_inc(pool_set, 1)
                    pool.wait_ge(pool_set, 5)
                    pool.tensor_tensor(gam[:], con[:, CO_E:CO_E + 1].to_broadcast([P, 2 * NPAIR + H]), edec[:], ALU.pow).then_inc(pool_set, 1)
                    pool.wait_ge(dve_set, 2)
                    for e in range(2):
                        for hp in range(NPAIR):
                            hd = NPAIR + 2 * hp + e
                            pool.tensor_tensor(dist_pow[:, e, hp, :], gam[:, hd:hd + 1].to_broadcast([P, C]), con[:, CO_DIST:CO_DIST + C], ALU.pow)
                    pool.memset(chunk_decay[:], float(C)).then_inc(pool_set, 1)
                    pool.wait_ge(pool_set, 7)
                    pool.tensor_tensor(chunk_decay[:], gam[:, DEC_PAIR], chunk_decay[:], ALU.pow).then_inc(pool_set, 1)

                @block.vector
                def _(dve):
                    dve.wait_ge(pool_set, 6)
                    dve.tensor_scalar(gam[:, 0:NPAIR + H], gam[:, 0:NPAIR + H], 1.0, None, ALU.add).then_inc(dve_set, 1)
                    dve.wait_ge(dve_set, 1)
                    dve.reciprocal(gam[:, 0:NPAIR + H], gam[:, 0:NPAIR + H]).then_inc(dve_set, 1)
                    dve.wait_ge(small_in, 4 * 16)
                    for h in range(NPAIR):
                        dve.tensor_scalar(wr_sb[:, h, :], wr_sb[:, h, :], gam[:, NPAIR + H + h:NPAIR + H + h + 1], None, ALU.mult)
                    for b in range(B):
                        lo_bank, hi_bank = duo[b % 2][:, 0, :], duo[b % 2][:, 1, :]
                        dve.wait_ge(pe_set, b + 1)
                        dve.tensor_copy(sa[:, b, :], lo_bank[:, 0:D])
                        dve.tensor_scalar(ca1[:, b, :], lo_bank[:, D:2 * D], 1.0, None, ALU.add)
                        dve.tensor_copy(ga[:, b, :], hi_bank[:, 0:D])
                        dve.tensor_copy(gbs[:, b, :], hi_bank[:, D:2 * D]).then_inc(dve_set, 1)
                    dve.wait_ge(pe_set, B + 1)
                    for k in range(KT):
                        dve.tensor_copy(sbm[:, k, :], mlp[0][:, B * k:B * k + B])
                        dve.tensor_scalar(cb1[:, k, :], mlp[0][:, B * (KT + k):B * (KT + k + 1)], 1.0, None, ALU.add)
                    dve.wait_ge(dve_set, 2 + B)
                    for k, g in enumerate((ga, gbs)):
                        dve.tensor_scalar(sgn[:, k], g[:], 0.0, 2.0, ALU.is_ge, ALU.mult)
                        dve.scalar_tensor_tensor(mag[:, k], g[:], -1.0, g[:], ALU.mult, ALU.max).then_inc(dve_set, 1)
                    dve.wait_ge(dve_set, 4 + B)
                    for k in range(2):
                        dve.tensor_scalar(sgn[:, k], sgn[:, k], -1.0, None, ALU.add)
                        dve.tensor_scalar(mag[:, k], mag[:, k], 0.25, None, ALU.max).then_inc(dve_set, 1)
                    dve.wait_ge(dve_set, 6 + B)
                    dve.tensor_tensor(ga[:], mag[:, 0], sgn[:, 0], ALU.mult)
                    dve.tensor_tensor(gbs[:], mag[:, 1], sgn[:, 1], ALU.mult).then_inc(dve_set, 1)
                    dve.wait_ge(dve_set, 7 + B)
                    for b in range(B):
                        dve.tensor_tensor(gbs[:, b, :], gbs[:, b, :], s3_sb[:], ALU.mult)
                    dve.wait_ge(pool_set, 8)
                    heads = [P, H, C]
                    flat_pow = dist_pow[:].rearrange("p e q n -> p (e q) n")
                    for k in range(LEVELS):
                        m = con[:, CO_MASK + k * C:CO_MASK + (k + 1) * C]
                        dve.tensor_tensor(level_mask[:, k].rearrange("p e q n -> p (e q) n"), flat_pow, m.unsqueeze(1).to_broadcast(heads), ALU.mult)
                    up = con[:, CO_UP:CO_UP + C].unsqueeze(1).to_broadcast([P, NPAIR, C])
                    for b in range(NB):
                        for e in range(2):
                            dve.tensor_tensor(intra_mask[:, e, b], dist_pow[:, e], up, ALU.mult)
                    for e in range(2):
                        for hp in range(NPAIR):
                            dve.tensor_copy(tail_decay[:, 2 * hp + e:2 * hp + e + 1], dist_pow[:, e, hp, C - 1:C])
                    dve.wait_ge(pe_set, B + 2)
                    for e in range(2):
                        for c in range(2):
                            row0 = solo[0][half(e), e * NPAIR * C:(e + 1) * NPAIR * C].rearrange("p (q n) -> p q n", n=C)
                            dve.tensor_copy(head_decay[half(e), :, c, :], row0)

                @block.tensor
                def _(pe):
                    pe.wait_ge(act_set, 2)
                    for b in range(B):
                        lo_bank, hi_bank = duo[b % 2][:, 0, :], duo[b % 2][:, 1, :]
                        if b >= 2:
                            pe.wait_ge(dve_set, 2 + b - 1)
                        for dst, col, n in ((lo_bank, 0, 2 * D), (hi_bank[:, 0:D], 2 * D, D), (hi_bank[:, D:2 * D], 5 * D, D)):
                            for k in range(KT):
                                mm = pe.matmul(dst, scB[:, k, b, :], wmod_sb[:, k, col:col + n], start=k == 0, stop=k == KT - 1)
                        mm.then_inc(pe_set, 1)
                    for q in range(2 * KT):
                        for k in range(KT):
                            mm = pe.matmul(mlp[0][:, B * q:B * q + B], wmod_sb[:, k, 3 * D + q * P:3 * D + (q + 1) * P],
                                           scT[:, k, :], start=k == 0, stop=k == KT - 1)
                    mm.then_inc(pe_set, 1)
                    pe.wait_ge(pool_set, 8)
                    pe.matmul(solo[0][:, 0:H * C], con[:, CO_ROW0:CO_ROW0 + P], dist_pow[:].rearrange("p e q n -> p (e q n)"),
                              start=True, stop=True).then_inc(pe_set, 1)

        main(nc, ctx, sb, sem, sems, locals())


def main(nc, ctx, sb, sem, sems, env):
    (x, wts, out, duo, solo, mlp, w_hi, wv_sb, wr_sb, con, scale_sb, ca1, sa, ga, gbs, cb1, sbm, level_mask, intra_mask,
     head_decay, tail_decay, chunk_decay, minus_half, flag_i, slot_max, state, rT, act_hi, act_lo, wst, lost) = (env[k] for k in (
        "x", "wts", "out", "duo", "solo", "mlp", "w_hi", "wv_sb", "wr_sb", "con", "scale_sb", "ca1", "sa", "ga", "gbs", "cb1", "sbm",
        "level_mask", "intra_mask", "head_decay", "tail_decay", "chunk_decay", "minus_half", "flag_i", "slot_max", "state", "rT",
        "act_hi", "act_lo", "wst", "lost"))
    const_in, wst_in, hi_done, lo_done, max_done, flag_col, flag_row, flag_max, flag_set = (env[k] for k in (
        "const_in", "wst_in", "hi_done", "lo_done", "max_done", "flag_col", "flag_row", "flag_max", "flag_set"))
    ident = con[:, CO_ID:CO_ID + P]

    xin = sb("xin", [NB, D])
    st1 = sb("st1", [NB, 6])
    mv1 = sb("mv1", [NB, 2])
    ve1 = sb("ve1", [NB])
    rstd1 = sb("rstd1", [NB])
    h = sb("h", [NB, D])
    r = sb("r", [NB, D])
    ss = sb("ss", [NB * H])
    ssm = sb("ssm", [NB * H])
    rinv = sb("rinv", [NB * H])
    gah = sb("gah", [NB, D])
    base = sb("base", [NB, D])
    hT = sb("hT", [KT, NB, P])
    v = sb("v", [NB, D])
    kg = sb("kg", [NP, 2, DH])
    gram = sb("gram", [2, NP, C])
    intra = sb("intra", [2, NP, C])
    rg = sb("rg", [NP, P])
    lv = [sb(f"lv{i}", [2, NP, C]) for i in range(2)]
    near = sb("near", [2 * NP, C])
    inv = sb("inv", [2 * NP, HB])
    inv_t = sb("inv_t", [2 * NP, HB])
    invT = sb("invT", [2, NP, C])
    mi = sb("mi", [2 * NP, HB])
    vn = sb("vn", [NP, 2, DH])
    o_state = sb("o_state", [NP, P])
    oT = sb("oT", [NP, P])
    x1 = [sb(f"x1_{i}", [NB, D]) for i in range(2)]
    st2 = sb("st2", [NB, 6])
    mv2 = sb("mv2", [NB, 2])
    ve2 = sb("ve2", [NB])
    rstd2 = sb("rstd2", [NB])
    xn2 = sb("xn2", [NB, D])
    h2 = sb("h2", [KT, NB, P])
    xh = sb("xh", [KT, TOK], F32R)
    xl = sb("xl", [KT, TOK], F32R)
    gate = [sb(f"gate{i}", [TOK]) for i in range(2)]
    full = [sb(f"full{i}", [TOK]) for i in range(2)]
    y = sb("y", [NB, D])
    w_full = sb("w_full", [SLOT, P])
    low_max = sb("low_max", [1])
    low_any = sb("low_any", [1])

    x_in = sem("x_in")
    ln1_stats, ln1_mv, ln1_ve, ln1_rstd = sem("ln1_stats"), sem("ln1_mv"), sem("ln1_ve"), sem("ln1_rstd")
    h_mid, h_ready, sq_ready, ss_ready = sem("h_mid"), sem("h_ready"), sem("sq_ready"), sem("ss_ready")
    ss_floor, rinv_ready, r_ready, gah_ready, base_ready = (sem(k) for k in (
        "ss_floor", "rinv_ready", "r_ready", "gah_ready", "base_ready"))
    hT_full, hT_ready, rT_full, rT_carry, rT_ready = (sem(k) for k in ("hT_full", "hT_ready", "rT_full", "rT_carry", "rT_ready"))
    v_full, v_ready, kg_full, kg_ready = sem("v_full"), sem("v_ready"), sem("kg_full"), sem("kg_ready")
    gram_full, gram_ready, intra_ready, rg_ready = (sem(k) for k in ("gram_full", "gram_ready", "intra_ready", "rg_ready"))
    near_ready = sem("near_ready")
    inv_sum, inv_ready, inv_t_ready, invT_ready = sem("inv_sum"), sems("inv_ready", LEVELS), sems("inv_t_ready", LEVELS), sems("invT_ready", LEVELS)
    lv_ready, mi_full, mi_ready, upd_full = (sems(k, LEVELS) for k in ("lv_ready", "mi_full", "mi_ready", "upd_full"))
    pred_full, u_ready, vn_full, vn_ready, ds_full, state_ready = (sems(k, 2) for k in (
        "pred_full", "u_ready", "vn_full", "vn_ready", "ds_full", "state_ready"))
    o_state_ready, oT_ready, ao_full, ao_scaled, x1_ready = sem("o_state_ready"), sem("oT_ready"), sem("ao_full"), sem("ao_scaled"), sem("x1_ready")
    ln2_stats, ln2_mv, ln2_ve, ln2_rstd, xn2_ready = (sem(k) for k in (
        "ln2_stats", "ln2_mv", "ln2_ve", "ln2_rstd", "xn2_ready"))
    h2T_full, h2_ready, xh_ready, xl_ready = sem("h2T_full"), sem("h2_ready"), sem("xh_ready"), sem("xl_ready")
    l_full, l_act, l_ready = sems("l_full", 3), sems("l_act", 3), sems("l_ready", 3)
    prod_ready, l1_hi = sem("prod_ready"), sem("l1_hi")
    y_full, y_mid, y_ready = sems("y_full", NB), sems("y_mid", NB), sem("y_ready")
    y_out = sem("y_out")
    w_in = sem("w_in")
    y_half = sems("y_half", NB)

    layers = [(name, m) for name in ("l1", "l2", "l3") for m in range(HK)]
    chain = [(name, k) for k in range(1, LEVELS) for name in ("mi", "upd")]
    chain += [(name, c) for c in range(2) for name in ("pred", "new", "state")] + [("attn_out", 0)]
    mixed = [("start", 0), ("ln2", 0), ("y", 0), ("values", 0), ("gram", 0), ("y", 1)]
    next_layer = iter(layers)
    for k, item in enumerate(chain):
        fill = 2 if k < HK // 2 else 0 if item == ("pred", 0) else 1
        mixed += [next(next_layer) for _ in range(fill)] + [item]
    mixed += list(next_layer) + [("norm2", 0)]

    def put_after(item, *new):
        at = mixed.index(item) + 1
        mixed[at:at] = new

    put_after(("l1", 1), ("turn", 0))
    put_after(("upd", 1), ("keys", 0))
    put_after(("upd", 2), ("intra", 0))
    for k in range(1, LEVELS - 1):
        put_after(("upd", k), ("turn", k))
    next_norm = {("turn", 2): "stats", ("turn", 3): "norm", ("turn", 4): "unit"}

    def walk(part, now_on, pre=None, split=None):
        has_att, has_mlp, has_y, has_next = now_on
        for name, k in mixed:
            if name == "y":
                if has_y:
                    part(name, k)
            elif name in ("l1", "l2", "l3"):
                slot = layers.index((name, k))
                if has_mlp:
                    part(name, k)
                elif split and slot < SLOTS:
                    split(slot)
            elif name == "ln2":
                if has_mlp:
                    part(name, k)
            elif has_att:
                part(name, k)
            if has_next and pre and (name, k) in next_norm:
                pre(next_norm[name, k])

    ALL = (True, True, True, True)

    def first_step(step):
        step(0, 0, 0, (True, False, False, True))

    def run(eng, step):
        step(1, 1, 0, (True, True, False, True))
        step(2, 0, 1, ALL)
        with eng.Fori(2, STEPS // 2) as i:
            step(2 * i - 1, 1, i - 1, ALL)
            step(2 * i, 0, i, ALL)
        step(STEPS - 1, 1, STEPS // 2 - 1, (True, True, True, False))
        step(STEPS, 0, STEPS // 2, (False, True, True, False))
        step(STEPS + 1, 1, STEPS // 2, (False, False, True, False))

    def after(eng, semaphore, value):
        if not isinstance(value, int) or value > 0:
            eng.wait_ge(semaphore, value)

    def tokens(dram, g, t):
        rows = slice(t * P, (t + 1) * P) if isinstance(t, int) else bass.ds(t * P, P)
        return dram[g * NB:(g + 1) * NB, rows, :].rearrange("b p d -> p b d")

    def pairs(ap):
        return ap.rearrange("p (q n) -> p q n", q=NP)

    def grams(e):
        return duo[1][:, e, 0:NP * (C + 1)].rearrange("p (q n) -> p q n", n=C + 1)

    def nth(n, k):
        return HK * n - (HK - 1 - k)

    blocks = [(q, c, e) for q in range(NP) for c, e in ((0, 0), (1, 1), (0, 1), (1, 0))]
    tiles = [(q, e, c) for e in range(2) for q in range(NP) for c in range(2)]

    def of_head(ap):
        return ap.rearrange("p (k n) -> p k n", n=HB)
    pair_of = [(b, hp) for b in range(NB) for hp in range(H // 2)]

    UNITS = 3 * HK + 2 * NB
    unit = {key: u for u, key in enumerate(layers)} | {("y", b): 3 * HK + 2 * b for b in range(NB)}

    def units_done(m, u):
        return UNITS * m - (UNITS - 1 - u)

    with nc.Block() as block:
        @block.sync
        def _(sp):
            def load(parts):
                for dst, blk, count in parts:
                    sp.dma_start(w_full[:, dst:dst + count, :],
                                 wts[blk // SLOT].rearrange("p (b n) -> p b n", n=P)[:, blk % SLOT:blk % SLOT + count, :]).then_inc(w_in, 32 // len(parts))

            def load_layers(m):
                for k in range(HK):
                    if k == 0:
                        after(sp, y_full[NB - 1], m - 1)
                    else:
                        sp.wait_ge(l_full[0], nth(m, k - 1))
                    load([(KT * i, w + KT * k, KT) for i, w in enumerate((BLK_W1, BLK_W2))])
                for i, w in ((1, BLK_H1), (2, BLK_H2)):
                    for k in range(HK):
                        if k == 0:
                            sp.wait_ge(l_full[i - 1], nth(m, HK - 1))
                        else:
                            sp.wait_ge(l_full[i], nth(m, k - 1))
                        load([(0, w + HK * k, HK)])

            def load_last(m):
                for k in range(NB):
                    if k == 0:
                        sp.wait_ge(l_full[2], nth(m, HK - 1))
                    else:
                        sp.wait_ge(y_full[k - 1], m)
                    load([(0, BLK_W3, SLOT)])
                    sp.wait_ge(y_half[k], m)
                    load([(0, BLK_W3 + SLOT, SLOT)])

            def program(general):
                run(sp, lambda *args: step(general, *args))

            def next_x(n, g, t):
                sp.wait_ge(base_ready, n + 1)
                sp.dma_start(xin[:], tokens(x, 1 - g, t + g)).then_inc(x_in, 16)

            def step(general, n, g, t, now_on):
                has_att, has_mlp, has_y, has_next = now_on
                if has_next:
                    next_x(n, g, t)
                if has_y:
                    if general:
                        load_last(n - 1)
                    sp.wait_ge(y_ready, n - 1)
                    sp.dma_start(tokens(out, g, t - 1), y[:]).then_inc(y_out, 16)
                if has_mlp and general:
                    load_layers(n)

            def load_slot(u, s):
                sp.wait_ge(lo_done, u - STAGES + 1)
                src = wts[u] if isinstance(u, int) else wts[bass.ds(u, 1)].rearrange("a p n -> (a p) n")
                sp.dma_start(wst[s][:], src).then_inc(wst_in[s], 16)

            sp.dma_start(xin[:], tokens(x, 0, 0)).then_inc(x_in, 16)
            next_x(0, 0, 0)
            with sp.Fori(1, SLOTS // STAGES) as i:
                for s in range(STAGES):
                    load_slot(STAGES * i + s, s)
            for u in range(SLOTS // STAGES * STAGES, SLOTS):
                load_slot(u, u % STAGES)
            sp.wait_ge(flag_set, 1)
            any_low = sp.value_load(flag_i[0:1, 0:1], min_val=0, max_val=1)
            with sp.If(any_low > 0):
                program(True)
            with sp.Else():
                program(False)
            sp.wait_ge(y_out, 16 * STEPS)

        @block.gpsimd
        def _(pool):
            def rsqrt(dst, src, done):
                pool.tensor_tensor(dst[:], src[:], minus_half[:, 0:src.shape[1]], ALU.pow).then_inc(done, 1)

            def pre(name, nxt):
                if name == "stats":
                    pool.wait_ge(ln1_ve, nxt)
                    rsqrt(rstd1, ve1, ln1_rstd)
                if name == "norm":
                    pool.wait_ge(ss_floor, nxt)
                    rsqrt(rinv, ssm, rinv_ready)

            def residual(g, nxt, now):
                pool.wait_ge(h_ready, nxt)
                pool.tensor_tensor(gah[:], h[:], ga[:, g * NB:(g + 1) * NB, :], ALU.mult).then_inc(gah_ready, 1)
                pool.wait_ge(gah_ready, nxt)
                if now is not None:
                    pool.wait_ge(x1_ready, now)
                pool.tensor_tensor(base[:], xin[:], gah[:], ALU.add).then_inc(base_ready, 1)

            def step(n, g, t, now_on):
                now, has_next = n + 1, now_on[3]

                def part(name, k):
                    if name == "start":
                        pool.wait_ge(rT_ready, now)
                        pool.tensor_tensor(rg[:].rearrange("p (b q) n -> p b q n", b=NB),
                                           rT[g][:, :, 1:P + 1].rearrange("p (b q) n -> p b q n", b=NB),
                                           head_decay[:].rearrange("p q c n -> p q (c n)").unsqueeze(1).to_broadcast([P, NB, H // 2, P]),
                                           ALU.mult).then_inc(rg_ready, 1)
                    if name == "gram" or (name == "mi" and k < LEVELS - 1):
                        level = k + 1
                        if level == 1:
                            pool.wait_ge(gram_ready, now)
                        if level >= 3:
                            pool.wait_ge(mi_full[level - 2], now)
                        pool.tensor_tensor(lv[level % 2][:].rearrange("p e (b q) n -> p e b (q n)", b=NB),
                                           gram[:].rearrange("p e (b q) n -> p e b (q n)", b=NB),
                                           level_mask[:, level].rearrange("p e q n -> p e (q n)").unsqueeze(2).to_broadcast([P, 2, NB, P]),
                                           ALU.mult).then_inc(lv_ready[level], 1)
                    if name == "attn_out":
                        pool.wait_ge(ln2_ve, now)
                        rsqrt(rstd2, ve2, ln2_rstd)
                        if has_next:
                            residual(1 - g, n + 2, now)

                walk(part, now_on, lambda name: pre(name, n + 2))

            pre("stats", 1)
            pre("norm", 1)
            residual(0, 1, None)
            first_step(step)
            run(pool, step)

        @block.scalar
        def _(act):
            def split(slot):
                act.wait_ge(wst_in[slot % STAGES], 16 * (slot // STAGES + 1))
                act.copy(w_hi[:, SLOT * slot:SLOT * (slot + 1), :].rearrange("p b n -> p (b n)"), wst[slot % STAGES][:]).then_inc(hi_done, 1)

            def step(n, g, t, now_on):
                now = n + 1

                def part(name, k):
                    if name == "start":
                        act.wait_ge(hT_full, now)
                        act.copy(hT[:].rearrange("p k b n -> p (k b n)"), duo[0][:, 0, :]).then_inc(hT_ready, 1)
                    if name == "values":
                        act.wait_ge(v_full, now)
                        act.copy(v[:].rearrange("p b n -> p (b n)"), solo[0][:]).then_inc(v_ready, 1)
                    if name == "gram":
                        act.wait_ge(gram_full, now)
                        for e in range(2):
                            ins = act.copy(gram[:, e], grams(e)[:, :, 0:C])
                        ins.then_inc(gram_ready, 1)
                    if name == "mi":
                        act.wait_ge(mi_full[k], now)
                        act.copy(mi[:].rearrange("p k n -> p (k n)"), duo[0][:, 0, 0:2 * NP * HB]).then_inc(mi_ready[k], 1)
                    if name == "turn":
                        act.wait_ge(inv_t_ready[k], now)
                        for i in range(2):
                            ins = act.activation(invT[:].rearrange("p e q n -> p (e q) n")[:, :, HB * i:HB * (i + 1)], inv_t[:],
                                                 ACT.Identity, scale=con[:, CO_BLK + i:CO_BLK + i + 1])
                        ins.then_inc(invT_ready[k], 1)
                    if name == "upd" and k == LEVELS - 1:
                        act.wait_ge(upd_full[k], now)
                        for c in range(2):
                            rows = slice(C * c, C * c + HB)
                            ins = act.activation(invT[rows].rearrange("p e q n -> p (e q) n")[:, :, HB:C], of_head(duo[0][rows, 1, 0:2 * NP * HB]),
                                                 ACT.Copy, scale=-1.0)
                        ins.then_inc(invT_ready[k], 1)
                    if name == "new":
                        act.wait_ge(vn_full[k], now)
                        act.copy(vn[half(k)].rearrange("p q e n -> p (q e n)"), solo[1][half(k), :]).then_inc(vn_ready[k], 1)
                    if name == "state" and k == 1:
                        act.wait_ge(ds_full[1], now)
                        act.copy(o_state[:].rearrange("p q n -> p (q n)"), duo[0][:, 1, :]).then_inc(o_state_ready, 1)
                    if name == "ln2":
                        act.wait_ge(h2T_full, n)
                        for kt in range(KT):
                            for b in range(NB):
                                ins = act.activation(h2[:, kt, b, :], solo[1][:, (kt * NB + b) * P:(kt * NB + b + 1) * P], ACT.Identity,
                                                     bias=sbm[:, kt, (1 - g) * NB + b:(1 - g) * NB + b + 1],
                                                     scale=cb1[:, kt, (1 - g) * NB + b:(1 - g) * NB + b + 1])
                        ins.then_inc(h2_ready, 1)
                    if name == "l1":
                        act.wait_ge(l_full[0], nth(n, k))
                        if k >= 2:
                            act.wait_ge(prod_ready, nth(n, k - 2))
                        act.activation(gate[k % 2][:], mlp[k % 2][:, 0:TOK], ACT.Silu,
                                       scale=scale_sb[:, 0, k:k + 1]).then_inc(l_act[0], 1)
                        for j in ([k - 1] if k > 0 else []) + ([k] if k == HK - 1 else []):
                            act.wait_ge(prod_ready, nth(n, j))
                            act.copy(act_hi[0][:, j, :], full[j % 2][:]).then_inc(l1_hi, 1)
                    if name in ("l2", "l3"):
                        layer = 1 if name == "l2" else 2
                        act.wait_ge(l_full[layer], nth(n, k))
                        if k >= 2:
                            act.wait_ge(l_ready[layer], nth(n, k - 2))
                        else:
                            act.wait_ge(l_ready[layer - 1], nth(n, HK - 2 + k))
                        s = scale_sb[:, layer + 1, k:k + 1]
                        act.activation(full[k % 2][:], mlp[k % 2][:, 0:TOK], ACT.Gelu, scale=s)
                        act.activation(act_hi[layer % 2][:, k, :], mlp[k % 2][:, 0:TOK], ACT.Gelu, scale=s).then_inc(l_act[layer], 1)

                walk(part, now_on, split=split if isinstance(n, int) and n == 0 else None)

            first_step(step)
            run(act, step)

        @block.vector
        def _(dve):
            def norm_stats(src, st, mv, ve, count, stats_done, mv_done, ve_done):
                for b in range(NB):
                    ins = dve.bn_stats(st[:, b, :], src[:, b, :])
                ins.then_inc(stats_done, 1)
                dve.wait_ge(const_in, 64)
                dve.wait_ge(stats_done, count)
                for b in range(NB):
                    ins = dve.bn_aggr(mv[:, b, :], st[:, b, :])
                ins.then_inc(mv_done, 1)
                dve.wait_ge(mv_done, count)
                dve.tensor_scalar(ve[:], mv[:, :, 1], EPS, None, ALU.add).then_inc(ve_done, 1)

            def pre(name, g, nxt):
                if name == "stats":
                    dve.wait_ge(x_in, 16 * nxt)
                    norm_stats(xin, st1, mv1, ve1, nxt, ln1_stats, ln1_mv, ln1_ve)
                if name == "norm":
                    dve.wait_ge(ln1_rstd, nxt)
                    after(dve, base_ready, nxt - 1)
                    for b in range(NB):
                        ins = dve.scalar_tensor_tensor(h[:, b, :], xin[:, b, :], mv1[:, b, 0:1], ca1[:, g * NB + b, :], ALU.subtract, ALU.mult)
                    ins.then_inc(h_mid, 1)
                    dve.wait_ge(h_mid, nxt)
                    for b in range(NB):
                        ins = dve.scalar_tensor_tensor(h[:, b, :], h[:, b, :], rstd1[:, b:b + 1], sa[:, g * NB + b, :], ALU.mult, ALU.add)
                    ins.then_inc(h_ready, 1)
                    dve.wait_ge(h_ready, nxt)
                    dve.tensor_tensor(r[:], h[:], h[:], ALU.mult).then_inc(sq_ready, 1)
                    dve.wait_ge(sq_ready, nxt)
                    dve.tensor_reduce(ss[:], r[:].rearrange("p b (h d) -> p (b h) d", h=H), AX.X, ALU.add).then_inc(ss_ready, 1)
                    dve.wait_ge(ss_ready, nxt)
                    dve.tensor_scalar(ssm[:], ss[:], 1e-24, None, ALU.max).then_inc(ss_floor, 1)
                if name == "unit":
                    dve.wait_ge(rinv_ready, nxt)
                    dve.tensor_tensor(r[:].rearrange("p b (h d) -> p (b h) d", h=H), h[:].rearrange("p b (h d) -> p (b h) d", h=H),
                                      rinv[:].unsqueeze(2).to_broadcast([P, NB * H, DH]), ALU.mult).then_inc(r_ready, 1)

            def split(slot):
                s = slot % STAGES
                dve.wait_ge(hi_done, slot + 1)
                dve.tensor_tensor(lost[s][:], wst[s][:], w_hi[:, SLOT * slot:SLOT * (slot + 1), :].bitcast(F32).rearrange("p b n -> p (b n)"),
                                  ALU.subtract).then_inc(lo_done, 1)
                dve.wait_ge(lo_done, slot + 1)
                dve.tensor_reduce(slot_max[:, slot:slot + 1], lost[s][:], AX.X, ALU.max, apply_absolute_value=True).then_inc(max_done, 1)

            def step(n, g, t, now_on):
                now = n + 1

                def low_part(layer, k):
                    dve.tensor_tensor(act_lo[layer % 2][:, k, :], full[k % 2][:], act_hi[layer % 2][:, k, :].bitcast(F32),
                                      ALU.subtract).then_inc(l_ready[layer], 1)

                def part(name, k):
                    if name == "start":
                        dve.wait_ge(rT_full, now)
                        dve.tensor_copy(rT[g][:, :, 0:1], rT[g][:, :, P:P + 1]).then_inc(rT_carry, 1)
                        dve.wait_ge(rT_carry, now)
                        dve.tensor_copy(rT[g][:, :, 1:P + 1], pairs(duo[0][:, 1, :])).then_inc(rT_ready, 1)
                    if name == "keys":
                        dve.wait_ge(kg_full, now)
                        dve.tensor_tensor(kg[:].rearrange("p (b q) e d -> p b (q e) d", b=NB),
                                          solo[1][:].rearrange("p (b h d) -> p b h d", b=NB, h=H),
                                          tail_decay[:].unsqueeze(1).unsqueeze(3).to_broadcast([P, NB, H, DH]), ALU.mult).then_inc(kg_ready, 1)
                    if name == "gram":
                        dve.wait_ge(gram_ready, now)
                        dve.tensor_tensor(near[:].rearrange("p (e b q) n -> p e b (q n)", e=2, b=NB),
                                          gram[:].rearrange("p e (b q) n -> p e b (q n)", b=NB),
                                          level_mask[:, 0].rearrange("p e q n -> p e (q n)").unsqueeze(2).to_broadcast([P, 2, NB, P]),
                                          ALU.mult).then_inc(near_ready, 1)
                        dve.wait_ge(near_ready, now)
                        dve.tensor_tensor(inv[:], near[:, :, 0:HB], near[:, :, HB:C], ALU.add).then_inc(inv_sum, 1)
                        dve.wait_ge(inv_sum, now)
                        dve.tensor_tensor(inv[:], inv[:], con[:, CO_EYE:CO_EYE + HB].unsqueeze(1).to_broadcast([P, 2 * NP, HB]), ALU.add).then_inc(inv_ready[0], 1)
                    if name == "upd" and k < LEVELS - 1:
                        dve.wait_ge(upd_full[k], now)
                        dve.tensor_tensor(inv[:], inv[:], of_head(duo[0][:, 1, 0:2 * NP * HB]), ALU.subtract).then_inc(inv_ready[k], 1)
                    if name == "turn":
                        dve.wait_ge(inv_ready[k], now)
                        dve.transpose(inv_t[:].rearrange("p k n -> p (k n)"), inv[:].rearrange("p k n -> p (k n)")).then_inc(inv_t_ready[k], 1)
                    if name == "intra":
                        for e in range(2):
                            ins = dve.tensor_tensor(intra[:, e], grams(e)[:, :, 1:C + 1], intra_mask[:, e].rearrange("p b q n -> p (b q) n"), ALU.mult)
                        ins.then_inc(intra_ready, 1)
                    if name == "pred":
                        if k == 0:
                            dve.wait_ge(v_ready, now)
                        dve.wait_ge(pred_full[k], now)
                        by_head = v[half(k)].rearrange("p b (q e d) -> p e (b q) d", e=2, d=DH)
                        dve.tensor_tensor(by_head, by_head, duo[1][half(k), :, 0:NP * DH].rearrange("p e (q d) -> p e q d", q=NP), ALU.subtract).then_inc(u_ready[k], 1)
                    if name == "state":
                        dve.wait_ge(ds_full[k], now)
                        s = state[g][:].rearrange("p (b q) d -> p q b d", b=NB)
                        ds = solo[0][:, 0:NP * DH].rearrange("p (b q d) -> p q b d", b=NB, d=DH)
                        for q in range(H // 2):
                            ins = dve.scalar_tensor_tensor(s[:, q], s[:, q], chunk_decay[:, q:q + 1], ds[:, q], ALU.mult, ALU.add)
                        ins.then_inc(state_ready[k], 1)
                        if k == 1:
                            dve.wait_ge(o_state_ready, now)
                            dve.tensor_tensor(oT[:].rearrange("p q n -> p (q n)"), o_state[:].rearrange("p q n -> p (q n)"),
                                              duo[0][:, 0, :], ALU.add).then_inc(oT_ready, 1)
                    if name == "attn_out":
                        xo = x1[g]
                        dve.wait_ge(ao_full, now)
                        dve.tensor_tensor(xo[:], duo[1][:, 0, :].rearrange("p (b n) -> p b n", b=NB),
                                          ga[:, g * NB:(g + 1) * NB, :], ALU.mult).then_inc(ao_scaled, 1)
                        dve.wait_ge(ao_scaled, now)
                        dve.wait_ge(base_ready, now)
                        dve.tensor_tensor(xo[:], xo[:], base[:], ALU.add).then_inc(x1_ready, 1)
                        dve.wait_ge(x1_ready, now)
                        norm_stats(xo, st2, mv2, ve2, now, ln2_stats, ln2_mv, ln2_ve)
                    if name == "norm2":
                        dve.wait_ge(ln2_rstd, now)
                        for b in range(NB):
                            ins = dve.tensor_scalar(xn2[:, b, :], x1[g][:, b, :], mv2[:, b, 0:1], rstd2[:, b:b + 1], ALU.subtract, ALU.mult)
                        ins.then_inc(xn2_ready, 1)
                    if name == "ln2":
                        dve.wait_ge(h2_ready, n)
                        flat = h2[:].rearrange("p k b n -> p k (b n)")
                        dve.tensor_copy(xh[:], flat).then_inc(xh_ready, 1)
                        dve.wait_ge(xh_ready, n)
                        dve.tensor_tensor(xl[:], flat, xh[:].bitcast(F32), ALU.subtract).then_inc(xl_ready, 1)
                    if name == "l1":
                        dve.wait_ge(l_act[0], nth(n, k))
                        if k >= 2:
                            dve.wait_ge(l_ready[0], nth(n, k - 2))
                        up, s = mlp[k % 2][:, TOK:2 * TOK], scale_sb[:, 1, k:k + 1]
                        dve.scalar_tensor_tensor(full[k % 2][:], up, s, gate[k % 2][:], ALU.mult, ALU.mult).then_inc(prod_ready, 1)
                        for j in ([k - 1] if k > 0 else []) + ([k] if k == HK - 1 else []):
                            dve.wait_ge(l1_hi, nth(n, j))
                            low_part(0, j)
                    if name in ("l2", "l3"):
                        layer = 1 if name == "l2" else 2
                        dve.wait_ge(l_act[layer], nth(n, k))
                        low_part(layer, k)
                    if name == "y":
                        m = n - 1
                        dve.wait_ge(y_full[k], m)
                        if k == 0:
                            after(dve, y_out, 16 * (m - 1))
                        dve.tensor_tensor(y[:, k, :], mlp[k][:, 0:D], gbs[:, g * NB + k, :], ALU.mult).then_inc(y_mid[k], 1)
                        dve.wait_ge(y_mid[k], m)
                        ins = dve.tensor_tensor(y[:, k, :], y[:, k, :], x1[g][:, k, :], ALU.add)
                        if k == NB - 1:
                            ins.then_inc(y_ready, 1)

                walk(part, now_on, lambda name: pre(name, 1 - g, n + 2), split if isinstance(n, int) and n == 0 else None)

            for name in ("stats", "norm", "unit"):
                pre(name, 0, 1)
            first_step(step)
            dve.wait_ge(max_done, SLOTS)
            dve.tensor_reduce(low_max[:], slot_max[:], AX.X, ALU.max).then_inc(flag_col, 1)
            dve.wait_ge(flag_row, 1)
            dve.tensor_reduce(low_any[0:1, :], mlp[1][0:1, 0:P], AX.X, ALU.max).then_inc(flag_max, 1)
            dve.wait_ge(flag_max, 1)
            dve.tensor_scalar(flag_i[0:1, :], low_any[0:1, :], 0.0, None, ALU.is_gt).then_inc(flag_set, 1)
            run(dve, step)

        @block.tensor
        def _(pe):
            def program(general):
                run(pe, lambda *args: step(general, *args))

            def step(general, n, g, t, now_on):
                now = n + 1

                def weights_in(m, u):
                    pe.wait_ge(w_in, 32 * units_done(m, u))

                def product(dst, w, parts, is_first, is_last):
                    for i, part in enumerate(parts):
                        general_ops = (w[1], part.bitcast(F32)) if general else (w[0], part)
                        mm = pe.matmul(dst, *general_ops, start=is_first and i == 0, stop=is_last and i == 1)
                    return mm

                def layer(name, k):
                    bank = mlp[k % 2]
                    if name == "l1":
                        if k == 0:
                            pe.wait_ge(xl_ready, n)
                            after(pe, y_mid[0], n - 1)
                        if k == 1:
                            after(pe, y_mid[1], n - 1)
                        if k >= 2:
                            pe.wait_ge(prod_ready, nth(n, k - 2))
                        if general:
                            weights_in(n, unit[name, k])
                        for i, w in enumerate((BLK_W1, BLK_W2)):
                            for j in range(KT):
                                mm = product(bank[:, i * TOK:(i + 1) * TOK], (w_hi[:, w + KT * k + j, :], w_full[:, KT * i + j, :]),
                                             (xh[:, j, :], xl[:, j, :]), j == 0, j == KT - 1)
                        mm.then_inc(l_full[0], 1)
                    if name in ("l2", "l3"):
                        i = 1 if name == "l2" else 2
                        hi, lo = act_hi[(i - 1) % 2], act_lo[(i - 1) % 2]
                        w = (BLK_H1 if i == 1 else BLK_H2) + HK * k
                        if k == 0:
                            pe.wait_ge(l_ready[i - 1], nth(n, HK - 2))
                        if k == 1:
                            pe.wait_ge(l_ready[i - 1], nth(n, HK - 1))
                        if k >= 2:
                            pe.wait_ge(l_act[i], nth(n, k - 2))
                        if general:
                            weights_in(n, unit[name, k])
                        for j in range(HK):
                            if k == 0:
                                pe.wait_ge(l_ready[i - 1], nth(n, j))
                            mm = product(bank[:, 0:TOK], (w_hi[:, w + j, :], w_full[:, j, :]), (hi[:, j, :], lo[:, j, :]), j == 0, j == HK - 1)
                        mm.then_inc(l_full[i], 1)

                def last_layer(k):
                    m = n - 1
                    hi, lo = act_hi[0], act_lo[0]
                    rows = slice(k * P, (k + 1) * P)
                    if k == 0:
                        pe.wait_ge(l_ready[2], nth(m, HK - 2))
                    for j in range(HK):
                        if k == 0:
                            pe.wait_ge(l_ready[2], nth(m, j))
                        u, first = unit["y", k] + j // (HK // 2), KT * (j % (HK // 2))
                        if general and first == 0:
                            weights_in(m, u)
                        w3 = w_hi[:, BLK_W3 + KT * j:BLK_W3 + KT * (j + 1), :].rearrange("p a n -> p (a n)")
                        w3_full = w_full[:, first:first + KT, :].rearrange("p a n -> p (a n)")
                        for i, part in enumerate((hi, lo)):
                            ops = (part[:, j, rows].bitcast(F32), w3_full) if general else (part[:, j, rows], w3)
                            mm = pe.matmul(mlp[k][:, 0:D], *ops, start=j == 0 and i == 0, stop=j == HK - 1 and i == 1)
                        if general and j == HK // 2 - 1:
                            mm.then_inc(y_half[k], 1)
                    mm.then_inc(y_full[k], 1)

                def part(name, k):
                    if name in ("l1", "l2", "l3"):
                        layer(name, k)
                    if name == "y":
                        last_layer(k)
                    if name == "start":
                        pe.wait_ge(h_ready, now)
                        for kt in range(KT):
                            for b in range(NB):
                                mm = pe.transpose(duo[0][:, 0, (kt * NB + b) * P:(kt * NB + b + 1) * P], h[:, b, kt * P:(kt + 1) * P], ident)
                        mm.then_inc(hT_full, 1)
                        pe.wait_ge(r_ready, now)
                        for q, (b, hp) in enumerate(pair_of):
                            mm = pe.transpose(duo[0][:, 1, q * P:(q + 1) * P], r[:, b, hp * P:(hp + 1) * P], ident)
                        mm.then_inc(rT_full, 1)
                    if name == "keys":
                        after(pe, h2_ready, n)
                        for q in range(NP):
                            mm = pe.transpose(solo[1][:, q * P:(q + 1) * P], rT[g][:, q, 0:P], ident)
                        mm.then_inc(kg_full, 1)
                    if name == "values":
                        pe.wait_ge(hT_ready, now)
                        for b in range(NB):
                            for kt in range(KT):
                                mm = pe.matmul(solo[0][:, b * D:(b + 1) * D], hT[:, kt, b, :], wv_sb[:, kt, :], start=kt == 0, stop=kt == KT - 1)
                        mm.then_inc(v_full, 1)
                    if name == "gram":
                        pe.wait_ge(const_in, 64)
                        pe.wait_ge(rT_ready, now)
                        for q, c, e in blocks:
                            keys = rT[g][half(e), q, C * c:C * c + C]
                            mm = pe.matmul(grams(e)[half(c), q, :], keys, rT[g][half(e), q, C * c:C * c + C + 1], start=True, stop=True)
                        mm.then_inc(gram_full, 1)
                    if name == "mi":
                        pe.wait_ge(const_in, 64)
                        pe.wait_ge(lv_ready[k], now)
                        pe.wait_ge(inv_ready[k - 1] if k < LEVELS - 1 else inv_t_ready[k - 1], now)
                        rhs = inv if k < LEVELS - 1 else inv_t
                        for q, e, c in tiles:
                            mm = pe.matmul(of_head(duo[0][half(c), 0, 0:2 * NP * HB])[:, e * NP + q, :], lv[k % 2][half(c), e, q, :],
                                           rhs[half(c), e * NP + q, :], start=True, stop=True)
                        mm.then_inc(mi_full[k], 1)
                    if name == "upd" and k < LEVELS - 1:
                        pe.wait_ge(const_in, 64)
                        pe.wait_ge(invT_ready[k - 1], now)
                        pe.wait_ge(mi_ready[k], now)
                        for q, e, c in tiles:
                            mm = pe.matmul(of_head(duo[0][half(c), 1, 0:2 * NP * HB])[:, e * NP + q, :], invT[half(c), e, q, :],
                                           mi[half(c), e * NP + q, :], start=True, stop=True)
                        mm.then_inc(upd_full[k], 1)
                    if name == "upd" and k == LEVELS - 1:
                        pe.wait_ge(const_in, 64)
                        pe.wait_ge(mi_ready[k], now)
                        for q, e, c in tiles:
                            rows = slice(C * c, C * c + HB)
                            mm = pe.matmul(of_head(duo[0][rows, 1, 0:2 * NP * HB])[:, e * NP + q, :], inv[rows, e * NP + q, :],
                                           mi[rows, e * NP + q, :], start=True, stop=True)
                        mm.then_inc(upd_full[k], 1)
                    if name == "pred":
                        pe.wait_ge(const_in, 64)
                        if k == 0:
                            pe.wait_ge(intra_ready, now)
                        else:
                            pe.wait_ge(state_ready[0], now)
                        for q in range(NP):
                            for e in range(2):
                                mm = pe.matmul(duo[1][half(k), e, q * DH:(q + 1) * DH], rT[g][half(e), q, C * k:C * k + C],
                                               state[g][half(e), q, :], start=True, stop=True)
                        mm.then_inc(pred_full[k], 1)
                    if name == "new":
                        pe.wait_ge(const_in, 64)
                        if k == 0:
                            pe.wait_ge(kg_ready, now)
                            pe.wait_ge(invT_ready[LEVELS - 1], now)
                        pe.wait_ge(u_ready[k], now)
                        for q, (b, hp) in enumerate(pair_of):
                            for e in range(2):
                                hd = hp * 2 + e
                                mm = pe.matmul(solo[1][half(k), q * P + DH * e:q * P + DH * e + DH], invT[half(k), e, q, :],
                                               v[half(k), b, hd * DH:(hd + 1) * DH], start=True, stop=True)
                        mm.then_inc(vn_full[k], 1)
                    if name == "state":
                        pe.wait_ge(const_in, 64)
                        if k == 0:
                            pe.wait_ge(rg_ready, now)
                        pe.wait_ge(vn_ready[k], now)
                        for q in range(NP):
                            for e in range(2):
                                cols = slice(q * P + C * k, q * P + C * k + C)
                                pe.matmul(duo[0][half(e), 1, cols], state[g][half(e), q, :], rg[half(e), q, C * k:C * k + C], start=True, stop=True)
                                pe.matmul(duo[0][half(e), 0, cols], vn[half(k), q, e, :], intra[half(k), e, q, :], start=True, stop=True)
                                mm = pe.matmul(solo[0][half(e), q * DH:(q + 1) * DH], kg[half(k), q, e, :], vn[half(k), q, e, :], start=True, stop=True)
                        mm.then_inc(ds_full[k], 1)
                    if name == "attn_out":
                        pe.wait_ge(oT_ready, now)
                        for b in range(NB):
                            for hp in range(H // 2):
                                mm = pe.matmul(duo[1][:, 0, b * D:(b + 1) * D], oT[:, b * (H // 2) + hp, :], wr_sb[:, hp, :],
                                               start=hp == 0, stop=hp == H // 2 - 1)
                        mm.then_inc(ao_full, 1)
                    if name == "ln2":
                        pe.wait_ge(xn2_ready, n)
                        for kt in range(KT):
                            for b in range(NB):
                                mm = pe.transpose(solo[1][:, (kt * NB + b) * P:(kt * NB + b + 1) * P], xn2[:, b, kt * P:(kt + 1) * P], ident)
                        mm.then_inc(h2T_full, 1)

                walk(part, now_on)

            first_step(lambda *args: step(False, *args))
            pe.wait_ge(flag_col, 1)
            pe.transpose(mlp[1][0:1, 0:P], low_max[:], ident).then_inc(flag_row, 1)
            pe.wait_ge(flag_set, 1)
            any_low = pe.value_load(flag_i[0:1, 0:1], min_val=0, max_val=1)
            with pe.If(any_low > 0):
                program(True)
            with pe.Else():
                program(False)


INPUTS = ("x", "wts", "wv", "wr", "wmod", "cT", "cB", "scales", "s3", "dec_pair", "dec_all", "alpha_pair", "const")


def kernel(**inputs):
    import concourse.bacc as bacc
    from concourse.bass_utils import run_bass_kernel_spmd

    a = {k[3:]: np.asarray(v) for k, v in inputs.items()}

    def turned(w):
        o, i = w.shape
        return w.reshape(o // P, P, i // P, P).transpose(3, 0, 2, 1).reshape(P, -1, P)

    w3 = a["ffn_w3_w"].reshape(KT, P, HK, P).transpose(3, 2, 0, 1).reshape(P, -1, P)
    blocks = np.concatenate([turned(a["ffn_w1_w"]), turned(a["ffn_w2_w"]), turned(a["ffn_h1_w"]), turned(a["ffn_h2_w"]), w3], 1)
    rows = lambda w: w.reshape(KT, P, -1).transpose(1, 0, 2)
    cT = rows(a["c"].T)
    pair = lambda z: np.repeat(z.reshape(H // 2, 2).T, C, axis=0)
    arrays = {
        "x": a["attn_out"],
        "wts": blocks.reshape(P, SLOTS, SLOT * P).transpose(1, 0, 2),
        "wv": rows(a["attn_Ww"].T),
        "wr": rows(a["attn_Wr"].T),
        "wmod": rows(a["wmod"]),
        "cT": cT,
        "cB": np.repeat(cT[:, :, :, None], P, axis=3),
        "scales": np.stack([a["ffn_" + k].reshape(HK, P).T for k in ("w1_s", "w2_s", "h1_s", "h2_s")], 1),
        "s3": np.repeat(a["ffn_w3_s"][None], P, axis=0),
        "dec_pair": pair(a["attn_decay"]),
        "dec_all": np.repeat(a["attn_decay"][None], P, axis=0),
        "alpha_pair": pair(a["attn_log_alpha"]),
        "const": constants(),
    }
    arrays = {k: np.ascontiguousarray(v) for k, v in arrays.items()}
    nc = bacc.Bacc("TRN2", target_bir_lowering=False, num_devices=1, dynamic_dma_scratch_size=1024)
    aps = [nc.dram_tensor(f"in_{k}", arrays[k].shape, F32, kind="ExternalInput").ap() for k in INPUTS]
    out = nc.dram_tensor("out_y", (B, T, D), F32, kind="ExternalOutput").ap()
    adaln_block(nc, *aps, out)
    r = run_bass_kernel_spmd(nc, [{f"in_{k}": arrays[k] for k in INPUTS}], core_ids=[0])
    return r.results[0]["out_y"]
```

```python
from contextlib import ExitStack

import numpy as np

import concourse.bass as bass
from concourse import mybir

F32 = mybir.dt.float32
F32R = mybir.dt.float32r
I32 = mybir.dt.int32
ACT = mybir.ActivationFunctionType
ALU = mybir.AluOpType
AX = mybir.AxisListType

P = 128
B, T, D = 4, 2048, 256
H, DH, C = 4, 64, 64
HID = 1024
KT = D // P
HK = HID // P
NB = 2
NG = B // NB
NP = NB * (H // 2)
STEPS = (T // P) * NG
TOK = NB * P
LEVELS = 6
HB = C // 2
EPS = 1e-5

BLK_W1, BLK_W2 = 0, HK * KT
BLK_H1 = BLK_W2 + HK * KT
BLK_H2 = BLK_H1 + HK * HK
BLK_W3 = BLK_H2 + HK * HK
BLOCKS = BLK_W3 + HK * KT
SLOT = 8
SLOTS = BLOCKS // SLOT
STAGES = 4
EARLY = 2 * STAGES

CO_ID, CO_EYE = 0, P
CO_MASK = CO_EYE + HB
CO_UP = CO_MASK + LEVELS * C
CO_DIST = CO_UP + C
CO_TURN = CO_DIST + 1
CO_ROW = CO_TURN + P
CO_BLK = CO_ROW + P
CO_E = CO_BLK + 2
CO_N = CO_E + 1


def constants():
    c = np.zeros((P, CO_N), np.float32)
    p = np.arange(P)[:, None]
    j, i = p % C, np.arange(C)[None, :]
    c[:, CO_ID:CO_ID + P] = np.eye(P)
    c[:, CO_EYE:CO_EYE + HB] = j % HB == np.arange(HB)[None, :]
    c[:, CO_MASK:CO_MASK + C] = -1.0 * ((j >> 1 == i >> 1) & (j > i))
    for k in range(1, LEVELS - 1):
        c[:, CO_MASK + k * C:CO_MASK + (k + 1) * C] = (
            (j >> (k + 1) == i >> (k + 1)) & ((i >> k) % 2 == 1) & ((j >> k) % 2 == 0))
    k = LEVELS - 1
    c[:, CO_MASK + k * C:CO_MASK + (k + 1) * C] = (j >= HB) & (i < HB)
    c[:, CO_UP:CO_UP + C] = i > j
    c[:, CO_DIST] = np.abs(p[:, 0] - (C - 1))
    c[:, CO_TURN:CO_TURN + P] = (p // C == p.T // C) & (j + j.T == C - 1)
    c[C - 1, CO_ROW:CO_ROW + P] = 1.0
    for k in range(2):
        c[:, CO_BLK + k] = j[:, 0] // HB == k
    c[:, CO_E] = np.e
    return c


def selectors():
    return np.repeat(np.eye(B, dtype=np.float32), P, axis=1)


def half(k):
    return slice(C * k, C * k + C)


def adaln_block(nc, x, wts, wv, wr, wmod, cT, scales, s3, decay, const, sel, out):
    pow_dram = nc.dram_tensor("decay_powers", (H, P), F32, kind="Internal").ap()
    with ExitStack() as ctx:
        def sb(name, shape, dt=F32, c=ctx):
            return c.enter_context(nc.sbuf_tensor(name, [P] + list(shape), dt))

        def sem(name):
            return ctx.enter_context(nc.semaphore(name))

        def sems(name, n):
            return [sem(f"{name}{i}") for i in range(n)]

        duo = [ctx.enter_context(nc.psum_tensor(f"duo{i}", [P, 2, 512], F32)) for i in range(2)]
        solo = [ctx.enter_context(nc.psum_tensor(f"solo{i}", [P, 512], F32)) for i in range(2)]
        mlp = [ctx.enter_context(nc.psum_tensor(f"mlp{i}", [P, 512], F32)) for i in range(2)]

        w_hi = sb("w_hi", [BLOCKS, P], F32R)
        wv_sb = sb("wv_sb", [KT, D])
        wr_sb = sb("wr_sb", [KT, D])
        con = sb("con", [CO_N])
        scale_sb = sb("scale_sb", [4, HK])
        mods = sb("mods", [B, 4, D])
        sa, ca1, ga, gbs = (mods[:, :, k, :] for k in range(4))
        cb1 = sb("cb1", [KT, B])
        sbm = sb("sbm", [KT, B])
        level_mask = sb("level_mask", [LEVELS, 2, H // 2, C])
        intra_mask = sb("intra_mask", [2, NB, H // 2, C])
        head_decay = sb("head_decay", [H // 2, 2, C])
        tail_decay = sb("tail_decay", [H])
        chunk_decay = sb("chunk_decay", [H // 2])
        minus_half = sb("minus_half", [NB * H])
        flag_i = sb("flag_i", [1], I32)
        state = [sb(f"state{g}", [NP, DH]) for g in range(NG)]
        rT = [sb(f"rT{g}", [NP, P + 1]) for g in range(NG)]
        xin = sb("xin", [NB, D])
        last = [sb(f"last{g}", [NB, D]) for g in range(NG)]
        with ExitStack() as early:
            wst = [sb(f"wst{s}", [SLOT * P], F32, early) for s in range(STAGES)]
            diff = sb("diff", [SLOT * P], F32, early)
        act_hi = [sb(f"act_hi{i}", [HK, TOK], F32R) for i in range(2)]
        act_lo = [sb(f"act_lo{i}", [HK, TOK], F32R) for i in range(2)]
        slot_diff = sb("slot_diff", [SLOTS])
        any_diff = sb("any_diff", [1])
        row_diff = sb("row_diff", [1])

        x_in = sem("x_in")
        decay_in, const_in, c_in, small_in, wst_in = sem("decay_in"), sem("const_in"), sem("c_in"), sem("small_in"), sems("wst_in", STAGES)
        hi_done, diff_done, row_done, gate_done, spread = sem("hi_done"), sem("diff_done"), sem("row_done"), sem("gate_done"), sems("spread", 2)
        exp_ready, gamma_mid, gamma_ready, pow_ready = sem("exp_ready"), sem("gamma_mid"), sem("gamma_ready"), sem("pow_ready")
        pow_turned, pow_row, pow_out, pow_in, pow_full = sem("pow_turned"), sem("pow_row"), sem("pow_out"), sem("pow_in"), sem("pow_full")
        flag_col, flag_row, flag_max, flag_set = sem("flag_col"), sem("flag_row"), sem("flag_max"), sem("flag_set")
        silu_done, mod_full, mod_spread, col_full = sem("silu_done"), sem("mod_full"), sem("mod_spread"), sem("col_full")
        pool_done = sem("pool_done")

        def load_slot(sp, u):
            if u >= STAGES:
                sp.wait_ge(diff_done, u - STAGES + 1)
            sp.dma_start(wst[u % STAGES][:], wts[u]).then_inc(wst_in[u % STAGES], 16)

        def high_part(act, u):
            act.wait_ge(wst_in[u % STAGES], 16 * (u // STAGES + 1))
            act.copy(w_hi[:, SLOT * u:SLOT * (u + 1), :], wst[u % STAGES][:].rearrange("p (b n) -> p b n", n=P)).then_inc(hi_done, 1)

        def differs(dve, u):
            dve.wait_ge(hi_done, u + 1)
            if u > 0:
                dve.wait_ge(diff_done, u)
            dve.scalar_tensor_tensor(diff[:], wst[u % STAGES][:], 1.0,
                                     w_hi[:, SLOT * u:SLOT * (u + 1), :].bitcast(F32).rearrange("p b n -> p (b n)"),
                                     ALU.mult, ALU.not_equal, accum_out=slot_diff[:, u:u + 1]).then_inc(diff_done, 1)

        with ExitStack() as tmp:
            wmod_sb = sb("wmod_sb", [KT, 6 * D], F32, tmp)
            cT_sb = sb("cT_sb", [KT, B], F32, tmp)
            scT = sb("scT", [KT, B], F32, tmp)
            s3_sb = sb("s3_sb", [D], F32, tmp)
            sel_sb = sb("sel_sb", [B, P], F32, tmp)
            row = sb("row", [4, D], F32, tmp)
            sgn = sb("sgn", [2, D], F32, tmp)
            mag = sb("mag", [2, D], F32, tmp)
            NPAIR = H // 2
            dec = sb("dec", [NPAIR + H + NPAIR], F32, tmp)
            gam = sb("gam", [NPAIR + H + NPAIR], F32, tmp)
            edec = sb("edec", [NPAIR + H + NPAIR], F32, tmp)
            powers = sb("powers", [H], F32, tmp)
            pow_row_sb = sb("pow_row_sb", [P], F32, tmp)
            hank = sb("hank", [H, C], F32, tmp)
            DEC_PAIR, DEC_ALL, DEC_ALPHA = slice(0, NPAIR), slice(NPAIR, NPAIR + H), slice(NPAIR + H, NPAIR + H + NPAIR)

            with nc.Block() as block:
                @block.sync
                def _(sp):
                    sp.dma_start(dec[:], decay).then_inc(decay_in, 16)
                    sp.dma_start(con[:], const).then_inc(const_in, 16)
                    sp.dma_start(xin[:], x[0:NB, 0:P, :].rearrange("b p d -> p b d")).then_inc(x_in, 16)
                    sp.dma_start(wst[0][:], wts[0]).then_inc(wst_in[0], 16)
                    sp.wait_ge(pow_row, 1)
                    sp.dma_start(pow_dram, pow_row_sb[0:H, :]).then_inc(pow_out, 16)
                    sp.dma_start(wst[1][:], wts[1]).then_inc(wst_in[1], 16)
                    sp.wait_ge(pow_out, 16)
                    for c in range(2):
                        shifted = bass.AP(pow_dram.tensor, pow_dram.offset, [[1, C], [P, H], [1, C]])
                        sp.dma_start(hank[half(c)], shifted).then_inc(pow_in, 16)
                    for s in range(2, STAGES):
                        sp.dma_start(wst[s][:], wts[s]).then_inc(wst_in[s], 16)
                    for u in range(STAGES, EARLY + STAGES):
                        load_slot(sp, u)

                @block.scalar
                def _(act):
                    for dst, src in ((cT_sb[:], cT), (wmod_sb[:], wmod)):
                        act.dma_start(dst, src).then_inc(c_in, 16)
                    for dst, src in ((s3_sb[0:B], s3), (sel_sb[0:B], sel.rearrange("b (a p) -> b a p", p=P)), (scale_sb[:], scales),
                                     (wv_sb[:], wv), (wr_sb[:], wr)):
                        act.dma_start(dst, src).then_inc(small_in, 16)
                    act.wait_ge(c_in, 2 * 16)
                    act.activation(scT[:], cT_sb[:], ACT.Silu).then_inc(silu_done, 1)
                    for u in range(EARLY // 2):
                        high_part(act, u)
                    for b in range(B):
                        act.wait_ge(mod_spread, b + 1)
                        act.copy(mods[:, b, 0:2, :], duo[b % 2][:, 0, :].rearrange("p (k d) -> p k d", k=2)).then_inc(spread[0], 1)
                        high_part(act, EARLY // 2 + b)

                @block.gpsimd
                def _(pool):
                    pool.wait_ge(decay_in, 16)
                    pool.wait_ge(const_in, 16)
                    pool.tensor_scalar(edec[:, 0:NPAIR + H], dec[:, 0:NPAIR + H], -1.0, None, ALU.mult).then_inc(pool_done, 1)
                    pool.tensor_copy(edec[:, DEC_ALPHA], dec[:, DEC_ALPHA]).then_inc(pool_done, 1)
                    pool.memset(chunk_decay[:], float(C)).then_inc(pool_done, 1)
                    pool.wait_ge(pool_done, 3)
                    pool.tensor_tensor(gam[:], con[:, CO_E:CO_E + 1].to_broadcast([P, 2 * NPAIR + H]), edec[:], ALU.pow).then_inc(exp_ready, 1)
                    pool.wait_ge(gamma_ready, 1)
                    pool.tensor_tensor(powers[:], gam[:, DEC_ALL], con[:, CO_DIST:CO_DIST + 1].to_broadcast([P, H]), ALU.pow).then_inc(pow_ready, 1)
                    pool.tensor_tensor(chunk_decay[:], gam[:, DEC_PAIR], chunk_decay[:], ALU.pow)
                    pool.memset(minus_half[:], -0.5)
                    for g in range(NG):
                        pool.memset(state[g][:], 0.0)
                        pool.memset(rT[g][:], 0.0)
                        pool.memset(last[g][0:1], 0.0)

                @block.vector
                def _(dve):
                    dve.wait_ge(exp_ready, 1)
                    dve.tensor_scalar(gam[:, 0:NPAIR + H], gam[:, 0:NPAIR + H], 1.0, None, ALU.add).then_inc(gamma_mid, 1)
                    dve.wait_ge(gamma_mid, 1)
                    dve.reciprocal(gam[:, 0:NPAIR + H], gam[:, 0:NPAIR + H]).then_inc(gamma_ready, 1)
                    dve.wait_ge(pow_turned, 1)
                    dve.tensor_copy(pow_row_sb[0:H, :], solo[1][0:H, 0:P]).then_inc(pow_row, 1)

                    def tables():
                        dve.wait_ge(pow_full, 2)
                        near_pow = solo[0][:, 0:H * C].rearrange("p (k n) -> p k n", n=C)
                        for k in range(LEVELS):
                            m = con[:, CO_MASK + k * C:CO_MASK + (k + 1) * C]
                            dve.tensor_tensor(level_mask[:, k].rearrange("p e q n -> p (e q) n"), near_pow, m.unsqueeze(1).to_broadcast([P, H, C]), ALU.mult)
                        up = con[:, CO_UP:CO_UP + C].unsqueeze(1).to_broadcast([P, NPAIR, C])
                        for e in range(2):
                            for b in range(NB):
                                dve.tensor_tensor(intra_mask[:, e, b], near_pow[:, e * NPAIR:(e + 1) * NPAIR, :], up, ALU.mult)
                            dve.tensor_copy(tail_decay[:].rearrange("p (q e) -> p e q", e=2)[:, e, :], near_pow[:, e * NPAIR:(e + 1) * NPAIR, C - 1])
                            for c in range(2):
                                row_pow = solo[1][half(e), e * NPAIR * C:(e + 1) * NPAIR * C].rearrange("p (q n) -> p q n", n=C)
                                dve.tensor_copy(head_decay[half(e), :, c, :], row_pow)

                    def modulation():
                        lo_bank, mid_bank, hi_bank = duo[0][0:B, 0, :], duo[0][0:B, 1, :], duo[1][0:B, 0, :]
                        dve.wait_ge(mod_full, 1)
                        dve.tensor_copy(row[0:B, 0, :], lo_bank[:, 0:D])
                        dve.tensor_scalar(row[0:B, 1, :], lo_bank[:, D:2 * D], 1.0, None, ALU.add)
                        dve.tensor_copy(row[0:B, 2, :], mid_bank[:, 0:D])
                        dve.tensor_copy(row[0:B, 3, :], hi_bank[:, D:2 * D]).then_inc(row_done, 1)
                        g = row[0:B, 2:4, :]
                        dve.wait_ge(row_done, 1)
                        dve.tensor_scalar(sgn[0:B], g, 0.0, 2.0, ALU.is_ge, ALU.mult)
                        dve.scalar_tensor_tensor(mag[0:B], g, -1.0, g, ALU.mult, ALU.max).then_inc(gate_done, 1)
                        dve.wait_ge(gate_done, 1)
                        dve.tensor_scalar(sgn[0:B], sgn[0:B], -1.0, None, ALU.add)
                        dve.tensor_scalar(mag[0:B], mag[0:B], 0.25, None, ALU.max).then_inc(gate_done, 1)
                        dve.wait_ge(gate_done, 2)
                        dve.tensor_tensor(g, mag[0:B], sgn[0:B], ALU.mult).then_inc(gate_done, 1)
                        dve.wait_ge(gate_done, 3)
                        dve.wait_ge(small_in, 5 * 16)
                        dve.tensor_tensor(row[0:B, 3, :], row[0:B, 3, :], s3_sb[0:B, :], ALU.mult).then_inc(gate_done, 1)
                        dve.wait_ge(col_full, 1)
                        for k in range(KT):
                            dve.tensor_copy(sbm[:, k, :], mlp[0][:, B * k:B * k + B])
                            dve.tensor_scalar(cb1[:, k, :], mlp[0][:, B * (KT + k):B * (KT + k + 1)], 1.0, None, ALU.add)

                    for u in range(2):
                        differs(dve, u)
                    modulation()
                    for u in range(2, EARLY // 2):
                        differs(dve, u)
                    tables()
                    for b in range(B):
                        dve.wait_ge(mod_spread, b + 1)
                        dve.tensor_copy(mods[:, b, 2:4, :], duo[b % 2][:, 1, :].rearrange("p (k d) -> p k d", k=2)).then_inc(spread[1], 1)
                        differs(dve, EARLY // 2 + b)
                    for h in range(NPAIR):
                        dve.tensor_scalar(wr_sb[:, h, :], wr_sb[:, h, :], gam[:, NPAIR + H + h:NPAIR + H + h + 1], None, ALU.mult)

                @block.tensor
                def _(pe):
                    pe.wait_ge(pow_ready, 1)
                    pe.transpose(solo[1][0:H, 0:P], powers[:], con[:, CO_ID:CO_ID + P]).then_inc(pow_turned, 1)
                    pe.wait_ge(silu_done, 1)
                    for i, bank in enumerate((duo[0][0:B, 0, :], duo[0][0:B, 1, :], duo[1][0:B, 0, :])):
                        for k in range(KT):
                            mm = pe.matmul(bank, scT[:, k, :], wmod_sb[:, k, 2 * D * i:2 * D * (i + 1)], start=k == 0, stop=k == KT - 1)
                    mm.then_inc(mod_full, 1)
                    for q in range(2 * KT):
                        for k in range(KT):
                            mm = pe.matmul(mlp[0][:, B * q:B * q + B], wmod_sb[:, k, 3 * D + q * P:3 * D + (q + 1) * P],
                                           scT[:, k, :], start=k == 0, stop=k == KT - 1)
                    mm.then_inc(col_full, 1)
                    pe.wait_ge(pow_in, 32)
                    flat = hank[:].rearrange("p h n -> p (h n)")
                    pe.matmul(solo[0][:, 0:H * C], con[:, CO_TURN:CO_TURN + P], flat, start=True, stop=True).then_inc(pow_full, 1)
                    pe.matmul(solo[1][:, 0:H * C], con[:, CO_ROW:CO_ROW + P], flat, start=True, stop=True).then_inc(pow_full, 1)
                    pe.wait_ge(gate_done, 4)
                    for b in range(B):
                        if b >= 2:
                            for i in range(2):
                                pe.wait_ge(spread[i], b - 1)
                        for i in range(2):
                            mm = pe.matmul(duo[b % 2][:, i, :], sel_sb[0:B, b, :], row[0:B, 2 * i:2 * i + 2, :].rearrange("p k d -> p (k d)"),
                                           start=True, stop=True)
                        mm.then_inc(mod_spread, 1)
        main(nc, ctx, sb, sem, sems, locals())


def main(nc, ctx, sb, sem, sems, env):
    (x, wts, out, duo, solo, mlp, w_hi, wv_sb, wr_sb, con, scale_sb, ca1, sa, ga, gbs, cb1, sbm, level_mask, intra_mask,
     head_decay, tail_decay, chunk_decay, minus_half, flag_i, state, rT, xin, last, act_hi, act_lo, slot_diff, any_diff, row_diff) = (env[k] for k in (
        "x", "wts", "out", "duo", "solo", "mlp", "w_hi", "wv_sb", "wr_sb", "con", "scale_sb", "ca1", "sa", "ga", "gbs", "cb1", "sbm",
        "level_mask", "intra_mask", "head_decay", "tail_decay", "chunk_decay", "minus_half", "flag_i", "state", "rT",
        "xin", "last", "act_hi", "act_lo", "slot_diff", "any_diff", "row_diff"))
    x_in, const_in, diff_done, flag_col, flag_row, flag_max, flag_set, load_slot, high_part, differs = (env[k] for k in (
        "x_in", "const_in", "diff_done", "flag_col", "flag_row", "flag_max", "flag_set", "load_slot", "high_part", "differs"))
    ident = con[:, CO_ID:CO_ID + P]

    st1 = sb("st1", [NB, 6])
    mv1 = sb("mv1", [NB, 2])
    ve1 = sb("ve1", [NB])
    rstd1 = sb("rstd1", [NB])
    h = sb("h", [NB, D])
    r = sb("r", [NB, D])
    ss = sb("ss", [NB * H])
    ssm = sb("ssm", [NB * H])
    rinv = sb("rinv", [NB * H])
    gah = sb("gah", [NB, D])
    base = sb("base", [NB, D])
    hT = sb("hT", [KT, NB, P])
    v = sb("v", [NB, D])
    kg = sb("kg", [NP, 2, DH])
    gram = sb("gram", [2, NP, C])
    intra = sb("intra", [2, NP, C])
    rg = sb("rg", [NP, P])
    lv = [sb(f"lv{i}", [2, NP, C]) for i in range(2)]
    near = lv[0][:].rearrange("p e q n -> p (e q) n")
    inv = sb("inv", [2 * NP, HB])
    inv_t = sb("inv_t", [2 * NP, HB])
    invT = sb("invT", [2, NP, C])
    mi = sb("mi", [2 * NP, HB])
    vn = sb("vn", [NP, 2, DH])
    o_state = sb("o_state", [NP, P])
    oT = sb("oT", [NP, P])
    x1 = [sb(f"x1_{i}", [NB, D]) for i in range(2)]
    st2 = sb("st2", [NB, 6])
    mv2 = sb("mv2", [NB, 2])
    ve2 = sb("ve2", [NB])
    rstd2 = sb("rstd2", [NB])
    xn2 = sb("xn2", [NB, D])
    h2 = sb("h2", [KT, NB, P])
    xh = sb("xh", [KT, TOK], F32R)
    xl = sb("xl", [KT, TOK], F32R)
    gate = [sb(f"gate{i}", [TOK]) for i in range(2)]
    full = [sb(f"full{i}", [TOK]) for i in range(2)]
    y = sb("y", [NB, D])
    unused = sb("unused", [1])
    w_full = sb("w_full", [SLOT, P])

    ln1_stats, ln1_mv, ln1_ve, ln1_rstd = sem("ln1_stats"), sem("ln1_mv"), sem("ln1_ve"), sem("ln1_rstd")
    h_mid, h_ready, sq_ready, ss_ready = sem("h_mid"), sem("h_ready"), sem("sq_ready"), sem("ss_ready")
    ss_floor, rinv_ready, r_ready, gah_ready, base_ready = (sem(k) for k in (
        "ss_floor", "rinv_ready", "r_ready", "gah_ready", "base_ready"))
    hT_full, hT_ready, rT_full, rT_carry, rT_ready = (sem(k) for k in ("hT_full", "hT_ready", "rT_full", "rT_carry", "rT_ready"))
    v_full, v_ready, kg_ready = sem("v_full"), sem("v_ready"), sem("kg_ready")
    keys_in, last_in = sem("keys_in"), sem("last_in")
    gram_full, intra_ready, rg_ready = sem("gram_full"), sem("intra_ready"), sem("rg_ready")
    near_ready, gram_ready, silu_loaded = sems("near_ready", 2), sems("gram_ready", 2), sem("silu_loaded")
    inv_sum, inv_ready, inv_t_ready, invT_ready = sem("inv_sum"), sems("inv_ready", LEVELS), sems("inv_t_ready", LEVELS), sem("invT_ready")
    diag_ready = sem("diag_ready")
    lv_ready, mi_full, mi_ready, upd_full = (sems(k, LEVELS) for k in ("lv_ready", "mi_full", "mi_ready", "upd_full"))
    pred_full, u_ready, vn_full, vn_ready, ds_full, state_ready = (sems(k, 2) for k in (
        "pred_full", "u_ready", "vn_full", "vn_ready", "ds_full", "state_ready"))
    o_state_ready, oT_ready, ao_full, ao_scaled, x1_ready = sem("o_state_ready"), sem("oT_ready"), sem("ao_full"), sem("ao_scaled"), sem("x1_ready")
    ln2_stats, ln2_mv, ln2_ve, ln2_rstd, xn2_ready = (sem(k) for k in (
        "ln2_stats", "ln2_mv", "ln2_ve", "ln2_rstd", "xn2_ready"))
    h2T_full, h2_ready, xh_ready, xl_ready = sem("h2T_full"), sem("h2_ready"), sem("xh_ready"), sem("xl_ready")
    l_full, l_act, l_ready = sems("l_full", 3), sems("l_act", 3), sems("l_ready", 3)
    prod_ready, l1_hi = sem("prod_ready"), sem("l1_hi")
    y_full, y_mid, y_ready = sems("y_full", NB), sems("y_mid", NB), sem("y_ready")
    y_out = sem("y_out")
    w_in = sem("w_in")
    y_half = sems("y_half", NB)

    layers = [(name, m) for name in ("l1", "l2", "l3") for m in range(HK)]
    chain = [(name, k) for k in range(1, LEVELS) for name in ("mi", "upd")]
    chain += [(name, c) for c in range(2) for name in ("pred", "new", "state")] + [("attn_out", 0)]
    mixed = [("start", 0), ("y", 0), ("ln2", 0), ("y", 1), ("gram", 0), ("values", 0), ("keys", 0)]
    FILL = {("mi", 1): 2, ("upd", 1): 2, ("mi", 2): 2, ("upd", 2): 2, ("pred", 0): 0}
    next_layer = iter(layers)
    for k, item in enumerate(chain):
        fill = FILL.get(item, 1)
        mixed += [next(next_layer) for _ in range(fill)] + [item]
    mixed += list(next_layer) + [("norm2", 0)]

    def put_after(item, *new):
        at = mixed.index(item) + 1
        mixed[at:at] = new

    put_after(("l1", 1), ("turn", 0))
    put_after(("upd", 2), ("intra", 0))
    for k in range(1, LEVELS - 1):
        put_after(("upd", k), ("turn", k))
    next_norm = {("turn", 2): "stats", ("turn", 3): "norm", ("mi", 4): "length", ("upd", 5): "unit"}

    slot_at = {layers[(len(layers) - 4) * i // (SLOTS - EARLY)]: EARLY + i for i in range(SLOTS - EARLY)}

    def walk(part, now_on, pre=None, split=None):
        has_att, has_mlp, has_y, has_next = now_on
        for name, k in mixed:
            if name == "y":
                if has_y:
                    part(name, k)
            elif name in ("l1", "l2", "l3", "ln2"):
                if has_mlp:
                    part(name, k)
                elif has_att and split and (name, k) in slot_at:
                    split(slot_at[name, k])
            elif has_att:
                part(name, k)
            if has_next and pre and (name, k) in next_norm:
                pre(next_norm[name, k])

    ALL = (True, True, True, True)

    def first_step(step):
        step(0, 0, 0, (True, False, False, True))

    def run(eng, step):
        step(1, 1, 0, (True, True, False, True))
        step(2, 0, 1, ALL)
        with eng.Fori(2, STEPS // 2) as i:
            step(2 * i - 1, 1, i - 1, ALL)
            step(2 * i, 0, i, ALL)
        step(STEPS - 1, 1, STEPS // 2 - 1, (True, True, True, False))
        step(STEPS, 0, STEPS // 2, (False, True, True, False))
        step(STEPS + 1, 1, STEPS // 2, (False, False, True, False))

    def after(eng, semaphore, value):
        if not isinstance(value, int) or value > 0:
            eng.wait_ge(semaphore, value)

    def tokens(dram, g, t):
        rows = slice(t * P, (t + 1) * P) if isinstance(t, int) else bass.ds(t * P, P)
        return dram[g * NB:(g + 1) * NB, rows, :].rearrange("b p d -> p b d")

    def pairs(ap):
        return ap.rearrange("p (q n) -> p q n", q=NP)

    def grams(e):
        return duo[1][:, e, 0:NP * (C + 1)].rearrange("p (q n) -> p q n", n=C + 1)

    def nth(n, k):
        return HK * n - (HK - 1 - k)

    blocks = [(q, c, e) for q in range(NP) for c, e in ((0, 0), (1, 1), (0, 1), (1, 0))]
    quarters = [(e, q, c, i) for e in range(2) for q in range(NP) for c in range(2) for i in range(2)]

    def quarter(c, i):
        return slice(C * c + HB * i, C * c + HB * i + HB)

    def of_head(ap):
        return ap.rearrange("p (k n) -> p k n", n=HB)

    pair_of = [(b, hp) for b in range(NB) for hp in range(H // 2)]

    UNITS = 3 * HK + 2 * NB
    unit = {key: u for u, key in enumerate(layers)} | {("y", b): 3 * HK + 2 * b for b in range(NB)}

    def units_done(m, u):
        return UNITS * m - (UNITS - 1 - u)

    with nc.Block() as block:
        @block.sync
        def _(sp):
            def load(parts):
                for dst, blk, count in parts:
                    sp.dma_start(w_full[:, dst:dst + count, :],
                                 wts[blk // SLOT].rearrange("p (b n) -> p b n", n=P)[:, blk % SLOT:blk % SLOT + count, :]).then_inc(w_in, 32 // len(parts))

            def load_layers(m):
                for k in range(HK):
                    if k == 0:
                        after(sp, y_full[NB - 1], m - 1)
                    else:
                        sp.wait_ge(l_full[0], nth(m, k - 1))
                    load([(KT * i, w + KT * k, KT) for i, w in enumerate((BLK_W1, BLK_W2))])
                for i, w in ((1, BLK_H1), (2, BLK_H2)):
                    for k in range(HK):
                        if k == 0:
                            sp.wait_ge(l_full[i - 1], nth(m, HK - 1))
                        else:
                            sp.wait_ge(l_full[i], nth(m, k - 1))
                        load([(0, w + HK * k, HK)])

            def load_last(m):
                for k in range(NB):
                    if k == 0:
                        sp.wait_ge(l_full[2], nth(m, HK - 1))
                    else:
                        sp.wait_ge(y_full[k - 1], m)
                    load([(0, BLK_W3, SLOT)])
                    sp.wait_ge(y_half[k], m)
                    load([(0, BLK_W3 + SLOT, SLOT)])

            def program(general):
                run(sp, lambda *args: step(general, *args))

            kg_rows = kg[:].rearrange("p (b q) e d -> p b (q e d)", b=NB)

            def keys(g):
                sp.dma_start(kg_rows[1:P], r[0:P - 1]).then_inc(keys_in, 16)
                sp.dma_start(kg_rows[0:1], last[g][0:1]).then_inc(keys_in, 16)

            def last_token(n, g):
                sp.wait_ge(kg_ready, n + 1)
                sp.dma_start(last[g][0:1], r[P - 1:P]).then_inc(last_in, 16)

            def step(general, n, g, t, now_on):
                has_att, has_mlp, has_y, has_next = now_on
                if has_att:
                    sp.wait_ge(base_ready, n + 1)
                    keys(g)
                if has_next:
                    sp.dma_start(xin[:], tokens(x, 1 - g, t + g)).then_inc(x_in, 16)
                if has_y:
                    if general:
                        load_last(n - 1)
                    sp.wait_ge(y_ready, n - 1)
                    sp.dma_start(tokens(out, g, t - 1), y[:]).then_inc(y_out, 16)
                if has_att:
                    last_token(n, g)
                if has_mlp and general:
                    load_layers(n)

            sp.wait_ge(r_ready, 1)
            keys(0)
            sp.wait_ge(base_ready, 1)
            sp.dma_start(xin[:], tokens(x, 1, 0)).then_inc(x_in, 16)
            last_token(0, 0)
            for u in range(EARLY + STAGES, SLOTS):
                load_slot(sp, u)
            sp.wait_ge(flag_set, 1)
            any_low = sp.value_load(flag_i[0:1, 0:1], min_val=0, max_val=1)
            with sp.If(any_low > 0):
                program(True)
            with sp.Else():
                program(False)
            sp.wait_ge(y_out, 16 * STEPS)

        @block.gpsimd
        def _(pool):
            def rsqrt(dst, src, done):
                pool.tensor_tensor(dst[:], src[:], minus_half[:, 0:src.shape[1]], ALU.pow).then_inc(done, 1)

            def pre(name, nxt):
                if name == "stats":
                    pool.wait_ge(ln1_ve, nxt)
                    rsqrt(rstd1, ve1, ln1_rstd)
                if name == "length":
                    pool.wait_ge(ss_floor, nxt)
                    rsqrt(rinv, ssm, rinv_ready)

            def residual(g, nxt, now):
                pool.wait_ge(h_ready, nxt)
                pool.tensor_tensor(gah[:], h[:], ga[:, g * NB:(g + 1) * NB, :], ALU.mult).then_inc(gah_ready, 1)
                pool.wait_ge(gah_ready, nxt)
                if now is not None:
                    pool.wait_ge(x1_ready, now)
                pool.tensor_tensor(base[:], xin[:], gah[:], ALU.add).then_inc(base_ready, 1)

            def step(n, g, t, now_on):
                now, has_next = n + 1, now_on[3]

                def part(name, k):
                    if name == "start":
                        pool.wait_ge(rT_ready, now)
                        pool.tensor_tensor(rg[:].rearrange("p (b q) n -> p b q n", b=NB),
                                           rT[g][:, :, 1:P + 1].rearrange("p (b q) n -> p b q n", b=NB),
                                           head_decay[:].rearrange("p q c n -> p q (c n)").unsqueeze(1).to_broadcast([P, NB, H // 2, P]),
                                           ALU.mult).then_inc(rg_ready, 1)
                    if name == "gram" or (name == "mi" and k < LEVELS - 1):
                        level = k + 1
                        if level == 2:
                            pool.wait_ge(inv_sum, now)
                        if level >= 3:
                            pool.wait_ge(mi_full[level - 2], now)
                        for e in range(2):
                            if level == 1:
                                pool.wait_ge(gram_ready[e], now)
                            ins = pool.tensor_tensor(lv[level % 2][:, e].rearrange("p (b q) n -> p b (q n)", b=NB),
                                                     gram[:, e].rearrange("p (b q) n -> p b (q n)", b=NB),
                                                     level_mask[:, level, e].rearrange("p q n -> p (q n)").unsqueeze(1).to_broadcast([P, NB, P]), ALU.mult)
                        ins.then_inc(lv_ready[level], 1)
                    if name == "attn_out":
                        pool.wait_ge(ln2_ve, now)
                        rsqrt(rstd2, ve2, ln2_rstd)
                        if has_next:
                            residual(1 - g, n + 2, now)

                walk(part, now_on, lambda name: pre(name, n + 2))

            pre("stats", 1)
            pre("length", 1)
            residual(0, 1, None)
            first_step(step)
            run(pool, step)

        @block.scalar
        def _(act):
            def step(n, g, t, now_on):
                now = n + 1

                def part(name, k):
                    if name == "start":
                        act.wait_ge(hT_full, now)
                        act.copy(hT[:].rearrange("p k b n -> p (k b n)"), duo[0][:, 0, :]).then_inc(hT_ready, 1)
                    if name == "values":
                        act.wait_ge(v_full, now)
                        act.copy(v[:].rearrange("p b n -> p (b n)"), solo[0][:]).then_inc(v_ready, 1)
                    if name == "gram":
                        act.wait_ge(gram_full, now)
                        for e in range(2):
                            if e == 1:
                                act.wait_ge(near_ready[0], now)
                            act.copy(gram[:, e], grams(e)[:, :, 0:C]).then_inc(gram_ready[e], 1)
                    if name == "mi":
                        act.wait_ge(mi_full[k], now)
                        act.copy(mi[:].rearrange("p k n -> p (k n)"), duo[0][:, 0, 0:2 * NP * HB]).then_inc(mi_ready[k], 1)
                    if name == "upd" and k == LEVELS - 1:
                        act.wait_ge(inv_t_ready[k - 1], now)
                        for i in range(2):
                            ins = act.activation(invT[:].rearrange("p e q n -> p (e q) n")[:, :, HB * i:HB * (i + 1)], inv_t[:],
                                                 ACT.Identity, scale=con[:, CO_BLK + i:CO_BLK + i + 1])
                        ins.then_inc(diag_ready, 1)
                        act.wait_ge(diag_ready, now)
                        act.wait_ge(upd_full[k], now)
                        for c in range(2):
                            ins = act.activation(invT[quarter(c, 0)].rearrange("p e q n -> p (e q) n")[:, :, HB:C],
                                                 of_head(duo[0][quarter(c, 0), 1, 0:2 * NP * HB]), ACT.Copy, scale=-1.0)
                        ins.then_inc(invT_ready, 1)
                    if name == "new":
                        act.wait_ge(vn_full[k], now)
                        act.copy(vn[half(k)].rearrange("p q e n -> p (q e n)"), solo[1][half(k), :]).then_inc(vn_ready[k], 1)
                    if name == "state" and k == 1:
                        act.wait_ge(ds_full[1], now)
                        act.copy(o_state[:].rearrange("p q n -> p (q n)"), duo[0][:, 1, :]).then_inc(o_state_ready, 1)
                    if name == "ln2":
                        act.wait_ge(h2T_full, n)
                        for kt in range(KT):
                            for b in range(NB):
                                ins = act.activation(h2[:, kt, b, :], solo[1][:, (kt * NB + b) * P:(kt * NB + b + 1) * P], ACT.Identity,
                                                     bias=sbm[:, kt, (1 - g) * NB + b:(1 - g) * NB + b + 1],
                                                     scale=cb1[:, kt, (1 - g) * NB + b:(1 - g) * NB + b + 1])
                        ins.then_inc(h2_ready, 1)
                    if name == "norm2":
                        after(act, silu_loaded, n)
                        act.activation(unused[:], con[:, CO_E:CO_E + 1], ACT.Silu).then_inc(silu_loaded, 1)
                    if name == "l1":
                        act.wait_ge(l_full[0], nth(n, k))
                        if k >= 2:
                            act.wait_ge(prod_ready, nth(n, k - 2))
                        act.activation(gate[k % 2][:], mlp[k % 2][:, 0:TOK], ACT.Silu,
                                       scale=scale_sb[:, 0, k:k + 1]).then_inc(l_act[0], 1)
                        for j in ([k - 1] if k > 0 else []) + ([k] if k == HK - 1 else []):
                            act.wait_ge(prod_ready, nth(n, j))
                            act.copy(act_hi[0][:, j, :], full[j % 2][:]).then_inc(l1_hi, 1)
                    if name in ("l2", "l3"):
                        layer = 1 if name == "l2" else 2
                        act.wait_ge(l_full[layer], nth(n, k))
                        if k >= 2:
                            act.wait_ge(l_ready[layer], nth(n, k - 2))
                        else:
                            act.wait_ge(l_ready[layer - 1], nth(n, HK - 2 + k))
                        s = scale_sb[:, layer + 1, k:k + 1]
                        act.activation(full[k % 2][:], mlp[k % 2][:, 0:TOK], ACT.Gelu, scale=s)
                        act.activation(act_hi[layer % 2][:, k, :], mlp[k % 2][:, 0:TOK], ACT.Gelu, scale=s).then_inc(l_act[layer], 1)

                walk(part, now_on, split=lambda slot: high_part(act, slot))

            first_step(step)
            run(act, step)

        @block.vector
        def _(dve):
            def norm_stats(src, st, mv, ve, count, stats_done, mv_done, ve_done):
                for b in range(NB):
                    ins = dve.bn_stats(st[:, b, :], src[:, b, :])
                ins.then_inc(stats_done, 1)
                dve.wait_ge(const_in, 16)
                dve.wait_ge(stats_done, count)
                for b in range(NB):
                    ins = dve.bn_aggr(mv[:, b, :], st[:, b, :])
                ins.then_inc(mv_done, 1)
                dve.wait_ge(mv_done, count)
                dve.tensor_scalar(ve[:], mv[:, :, 1], EPS, None, ALU.add).then_inc(ve_done, 1)

            def pre(name, g, nxt):
                if name == "stats":
                    dve.wait_ge(x_in, 16 * nxt)
                    norm_stats(xin, st1, mv1, ve1, nxt, ln1_stats, ln1_mv, ln1_ve)
                if name == "norm":
                    dve.wait_ge(ln1_rstd, nxt)
                    after(dve, base_ready, nxt - 1)
                    for b in range(NB):
                        ins = dve.scalar_tensor_tensor(h[:, b, :], xin[:, b, :], mv1[:, b, 0:1], ca1[:, g * NB + b, :], ALU.subtract, ALU.mult)
                    ins.then_inc(h_mid, 1)
                    dve.wait_ge(h_mid, nxt)
                    for b in range(NB):
                        ins = dve.scalar_tensor_tensor(h[:, b, :], h[:, b, :], rstd1[:, b:b + 1], sa[:, g * NB + b, :], ALU.mult, ALU.add)
                    ins.then_inc(h_ready, 1)
                    dve.wait_ge(h_ready, nxt)
                    after(dve, last_in, 16 * (nxt - 1))
                    dve.tensor_tensor(r[:], h[:], h[:], ALU.mult).then_inc(sq_ready, 1)
                    dve.wait_ge(sq_ready, nxt)
                    dve.tensor_reduce(ss[:], r[:].rearrange("p b (h d) -> p (b h) d", h=H), AX.X, ALU.add).then_inc(ss_ready, 1)
                    dve.wait_ge(ss_ready, nxt)
                    dve.tensor_scalar(ssm[:], ss[:], 1e-24, None, ALU.max).then_inc(ss_floor, 1)
                if name == "unit":
                    dve.wait_ge(rinv_ready, nxt)
                    dve.tensor_tensor(r[:].rearrange("p b (h d) -> p (b h) d", h=H), h[:].rearrange("p b (h d) -> p (b h) d", h=H),
                                      rinv[:].unsqueeze(2).to_broadcast([P, NB * H, DH]), ALU.mult).then_inc(r_ready, 1)

            def step(n, g, t, now_on):
                now = n + 1

                def low_part(layer, k):
                    dve.tensor_tensor(act_lo[layer % 2][:, k, :], full[k % 2][:], act_hi[layer % 2][:, k, :].bitcast(F32),
                                      ALU.subtract).then_inc(l_ready[layer], 1)

                def part(name, k):
                    if name == "start":
                        dve.wait_ge(rT_full, now)
                        dve.tensor_copy(rT[g][:, :, 0:1], rT[g][:, :, P:P + 1]).then_inc(rT_carry, 1)
                        dve.wait_ge(rT_carry, now)
                        dve.tensor_copy(rT[g][:, :, 1:P + 1], pairs(duo[0][:, 1, :])).then_inc(rT_ready, 1)
                    if name == "keys":
                        dve.wait_ge(keys_in, 32 * now)
                        by_head = kg[:].rearrange("p (b q) e d -> p b (q e) d", b=NB)
                        dve.tensor_tensor(by_head, by_head,
                                          tail_decay[:].unsqueeze(1).unsqueeze(3).to_broadcast([P, NB, H, DH]), ALU.mult).then_inc(kg_ready, 1)
                    if name == "gram":
                        dve.wait_ge(gram_full, now)
                        for i, e in enumerate((1, 0)):
                            if i == 1:
                                dve.wait_ge(gram_ready[0], now)
                            dve.tensor_tensor(near[:, e * NP:(e + 1) * NP, :].rearrange("p (b q) n -> p b q n", b=NB),
                                              grams(e)[:, :, 0:C].rearrange("p (b q) n -> p b q n", b=NB),
                                              level_mask[:, 0, e].unsqueeze(1).to_broadcast([P, NB, H // 2, C]), ALU.mult).then_inc(near_ready[i], 1)
                        dve.wait_ge(near_ready[1], now)
                        dve.tensor_tensor(inv[:], near[:, :, 0:HB], near[:, :, HB:C], ALU.add).then_inc(inv_sum, 1)
                        dve.wait_ge(inv_sum, now)
                        dve.tensor_tensor(inv[:], inv[:], con[:, CO_EYE:CO_EYE + HB].unsqueeze(1).to_broadcast([P, 2 * NP, HB]), ALU.add).then_inc(inv_ready[0], 1)
                    if name == "upd" and k < LEVELS - 1:
                        dve.wait_ge(upd_full[k], now)
                        dve.tensor_tensor(inv[:], inv[:], of_head(duo[0][:, 1, 0:2 * NP * HB]), ALU.subtract).then_inc(inv_ready[k], 1)
                    if name == "turn":
                        dve.wait_ge(inv_ready[k], now)
                        dve.transpose(inv_t[:].rearrange("p k n -> p (k n)"), inv[:].rearrange("p k n -> p (k n)")).then_inc(inv_t_ready[k], 1)
                    if name == "intra":
                        dve.wait_ge(gram_ready[1], now)
                        for e in range(2):
                            ins = dve.tensor_tensor(intra[:, e], grams(e)[:, :, 1:C + 1], intra_mask[:, e].rearrange("p b q n -> p (b q) n"), ALU.mult)
                        ins.then_inc(intra_ready, 1)
                    if name == "pred":
                        if k == 0:
                            dve.wait_ge(v_ready, now)
                        dve.wait_ge(pred_full[k], now)
                        by_head = v[half(k)].rearrange("p b (q e d) -> p e (b q) d", e=2, d=DH)
                        dve.tensor_tensor(by_head, by_head, duo[1][half(k), :, 0:NP * DH].rearrange("p e (q d) -> p e q d", q=NP), ALU.subtract).then_inc(u_ready[k], 1)
                    if name == "state":
                        dve.wait_ge(ds_full[k], now)
                        s = state[g][:].rearrange("p (b q) d -> p q b d", b=NB)
                        ds = solo[0][:, 0:NP * DH].rearrange("p (b q d) -> p q b d", b=NB, d=DH)
                        for q in range(H // 2):
                            ins = dve.scalar_tensor_tensor(s[:, q], s[:, q], chunk_decay[:, q:q + 1], ds[:, q], ALU.mult, ALU.add)
                        ins.then_inc(state_ready[k], 1)
                        if k == 1:
                            dve.wait_ge(o_state_ready, now)
                            dve.tensor_tensor(oT[:].rearrange("p q n -> p (q n)"), o_state[:].rearrange("p q n -> p (q n)"),
                                              duo[0][:, 0, :], ALU.add).then_inc(oT_ready, 1)
                    if name == "attn_out":
                        xo = x1[g]
                        dve.wait_ge(ao_full, now)
                        dve.tensor_tensor(xo[:], duo[1][:, 0, :].rearrange("p (b n) -> p b n", b=NB),
                                          ga[:, g * NB:(g + 1) * NB, :], ALU.mult).then_inc(ao_scaled, 1)
                        dve.wait_ge(ao_scaled, now)
                        dve.wait_ge(base_ready, now)
                        dve.tensor_tensor(xo[:], xo[:], base[:], ALU.add).then_inc(x1_ready, 1)
                        dve.wait_ge(x1_ready, now)
                        norm_stats(xo, st2, mv2, ve2, now, ln2_stats, ln2_mv, ln2_ve)
                    if name == "norm2":
                        dve.wait_ge(ln2_rstd, now)
                        for b in range(NB):
                            ins = dve.tensor_scalar(xn2[:, b, :], x1[g][:, b, :], mv2[:, b, 0:1], rstd2[:, b:b + 1], ALU.subtract, ALU.mult)
                        ins.then_inc(xn2_ready, 1)
                    if name == "ln2":
                        dve.wait_ge(h2_ready, n)
                        flat = h2[:].rearrange("p k b n -> p k (b n)")
                        dve.tensor_copy(xh[:], flat).then_inc(xh_ready, 1)
                        dve.wait_ge(xh_ready, n)
                        dve.tensor_tensor(xl[:], flat, xh[:].bitcast(F32), ALU.subtract).then_inc(xl_ready, 1)
                    if name == "l1":
                        dve.wait_ge(l_act[0], nth(n, k))
                        if k >= 2:
                            dve.wait_ge(l_ready[0], nth(n, k - 2))
                        up, s = mlp[k % 2][:, TOK:2 * TOK], scale_sb[:, 1, k:k + 1]
                        dve.scalar_tensor_tensor(full[k % 2][:], up, s, gate[k % 2][:], ALU.mult, ALU.mult).then_inc(prod_ready, 1)
                        for j in ([k - 1] if k > 0 else []) + ([k] if k == HK - 1 else []):
                            dve.wait_ge(l1_hi, nth(n, j))
                            low_part(0, j)
                    if name in ("l2", "l3"):
                        layer = 1 if name == "l2" else 2
                        dve.wait_ge(l_act[layer], nth(n, k))
                        low_part(layer, k)
                    if name == "y":
                        m = n - 1
                        dve.wait_ge(y_full[k], m)
                        if k == 0:
                            after(dve, y_out, 16 * (m - 1))
                        dve.tensor_tensor(y[:, k, :], mlp[k][:, 0:D], gbs[:, g * NB + k, :], ALU.mult).then_inc(y_mid[k], 1)
                        dve.wait_ge(y_mid[k], m)
                        ins = dve.tensor_tensor(y[:, k, :], y[:, k, :], x1[g][:, k, :], ALU.add)
                        if k == NB - 1:
                            ins.then_inc(y_ready, 1)

                walk(part, now_on, lambda name: pre(name, 1 - g, n + 2), lambda slot: differs(dve, slot))

            for name in ("stats", "norm", "unit"):
                pre(name, 0, 1)
            first_step(step)
            dve.wait_ge(diff_done, SLOTS)
            dve.tensor_reduce(any_diff[:], slot_diff[:], AX.X, ALU.max).then_inc(flag_col, 1)
            dve.wait_ge(flag_row, 1)
            dve.tensor_reduce(row_diff[0:1, :], mlp[1][0:1, 0:P], AX.X, ALU.max).then_inc(flag_max, 1)
            dve.wait_ge(flag_max, 1)
            dve.tensor_scalar(flag_i[0:1, :], row_diff[0:1, :], 0.0, None, ALU.is_gt).then_inc(flag_set, 1)
            run(dve, step)

        @block.tensor
        def _(pe):
            def program(general):
                run(pe, lambda *args: step(general, *args))

            def step(general, n, g, t, now_on):
                now = n + 1

                def weights_in(m, u):
                    pe.wait_ge(w_in, 32 * units_done(m, u))

                def product(dst, w, parts, is_first, is_last):
                    for i, part in enumerate(parts):
                        general_ops = (w[1], part.bitcast(F32)) if general else (w[0], part)
                        mm = pe.matmul(dst, *general_ops, start=is_first and i == 0, stop=is_last and i == 1)
                    return mm

                def layer(name, k):
                    bank = mlp[k % 2]
                    if name == "l1":
                        if k == 0:
                            pe.wait_ge(xl_ready, n)
                            after(pe, y_mid[0], n - 1)
                        if k == 1:
                            after(pe, y_mid[1], n - 1)
                        if k >= 2:
                            pe.wait_ge(prod_ready, nth(n, k - 2))
                        if general:
                            weights_in(n, unit[name, k])
                        for i, w in enumerate((BLK_W1, BLK_W2)):
                            for j in range(KT):
                                mm = product(bank[:, i * TOK:(i + 1) * TOK], (w_hi[:, w + KT * k + j, :], w_full[:, KT * i + j, :]),
                                             (xh[:, j, :], xl[:, j, :]), j == 0, j == KT - 1)
                        mm.then_inc(l_full[0], 1)
                    if name in ("l2", "l3"):
                        i = 1 if name == "l2" else 2
                        hi, lo = act_hi[(i - 1) % 2], act_lo[(i - 1) % 2]
                        w = (BLK_H1 if i == 1 else BLK_H2) + HK * k
                        if k < 2:
                            pe.wait_ge(prod_ready if i == 1 else l_act[i - 1], nth(n, HK - 2 + k))
                        if k >= 2:
                            pe.wait_ge(l_act[i], nth(n, k - 2))
                        if general:
                            weights_in(n, unit[name, k])
                        for j in range(HK):
                            if k == 0:
                                pe.wait_ge(l_ready[i - 1], nth(n, j))
                            mm = product(bank[:, 0:TOK], (w_hi[:, w + j, :], w_full[:, j, :]), (hi[:, j, :], lo[:, j, :]), j == 0, j == HK - 1)
                        mm.then_inc(l_full[i], 1)

                def last_layer(k):
                    m = n - 1
                    hi, lo = act_hi[0], act_lo[0]
                    rows = slice(k * P, (k + 1) * P)
                    if k == 0:
                        pe.wait_ge(l_act[2], nth(m, HK - 2))
                    for j in range(HK):
                        if k == 0:
                            pe.wait_ge(l_ready[2], nth(m, j))
                        u, first = unit["y", k] + j // (HK // 2), KT * (j % (HK // 2))
                        if general and first == 0:
                            weights_in(m, u)
                        w3 = w_hi[:, BLK_W3 + KT * j:BLK_W3 + KT * (j + 1), :].rearrange("p a n -> p (a n)")
                        w3_full = w_full[:, first:first + KT, :].rearrange("p a n -> p (a n)")
                        for i, part in enumerate((hi, lo)):
                            ops = (part[:, j, rows].bitcast(F32), w3_full) if general else (part[:, j, rows], w3)
                            mm = pe.matmul(mlp[k][:, 0:D], *ops, start=j == 0 and i == 0, stop=j == HK - 1 and i == 1)
                        if general and j == HK // 2 - 1:
                            mm.then_inc(y_half[k], 1)
                    mm.then_inc(y_full[k], 1)

                def part(name, k):
                    if name in ("l1", "l2", "l3"):
                        layer(name, k)
                    if name == "y":
                        last_layer(k)
                    if name == "start":
                        pe.wait_ge(h_ready, now)
                        for kt in range(KT):
                            for b in range(NB):
                                mm = pe.transpose(duo[0][:, 0, (kt * NB + b) * P:(kt * NB + b + 1) * P], h[:, b, kt * P:(kt + 1) * P], ident)
                        mm.then_inc(hT_full, 1)
                        pe.wait_ge(r_ready, now)
                        for q, (b, hp) in enumerate(pair_of):
                            mm = pe.transpose(duo[0][:, 1, q * P:(q + 1) * P], r[:, b, hp * P:(hp + 1) * P], ident)
                        mm.then_inc(rT_full, 1)
                    if name == "values":
                        pe.wait_ge(hT_ready, now)
                        for b in range(NB):
                            for kt in range(KT):
                                mm = pe.matmul(solo[0][:, b * D:(b + 1) * D], hT[:, kt, b, :], wv_sb[:, kt, :], start=kt == 0, stop=kt == KT - 1)
                        mm.then_inc(v_full, 1)
                    if name == "gram":
                        pe.wait_ge(const_in, 16)
                        pe.wait_ge(rT_ready, now)
                        for q, c, e in blocks:
                            keys = rT[g][half(e), q, C * c:C * c + C]
                            mm = pe.matmul(grams(e)[half(c), q, :], keys, rT[g][half(e), q, C * c:C * c + C + 1], start=True, stop=True)
                        mm.then_inc(gram_full, 1)
                    if name == "mi":
                        pe.wait_ge(const_in, 16)
                        pe.wait_ge(lv_ready[k], now)
                        pe.wait_ge(inv_ready[k - 1] if k < LEVELS - 1 else inv_t_ready[k - 1], now)
                        for e, q, c, i in quarters:
                            if k < LEVELS - 1:
                                rows = quarter(c, i)
                                mm = pe.matmul(of_head(duo[0][rows, 0, 0:2 * NP * HB])[:, e * NP + q, :], lv[k % 2][rows, e, q, HB * i:HB * (i + 1)],
                                               inv[rows, e * NP + q, :], start=True, stop=True)
                            elif i == 1:
                                mm = pe.matmul(of_head(duo[0][quarter(c, 0), 0, 0:2 * NP * HB])[:, e * NP + q, :], lv[k % 2][quarter(c, 1), e, q, 0:HB],
                                               inv_t[quarter(c, 1), e * NP + q, :], start=True, stop=True)
                        mm.then_inc(mi_full[k], 1)
                    if name == "upd":
                        pe.wait_ge(const_in, 16)
                        if k < LEVELS - 1:
                            pe.wait_ge(inv_t_ready[k - 1], now)
                        pe.wait_ge(mi_ready[k], now)
                        left = inv_t if k < LEVELS - 1 else inv
                        for e, q, c, i in quarters:
                            rows = quarter(c, i)
                            if k < LEVELS - 1 or i == 0:
                                mm = pe.matmul(of_head(duo[0][rows, 1, 0:2 * NP * HB])[:, e * NP + q, :], left[rows, e * NP + q, :],
                                               mi[rows, e * NP + q, :], start=True, stop=True)
                        mm.then_inc(upd_full[k], 1)
                    if name == "pred":
                        pe.wait_ge(const_in, 16)
                        if k == 0:
                            pe.wait_ge(intra_ready, now)
                        else:
                            pe.wait_ge(state_ready[0], now)
                        for q in range(NP):
                            for e in range(2):
                                mm = pe.matmul(duo[1][half(k), e, q * DH:(q + 1) * DH], rT[g][half(e), q, C * k:C * k + C],
                                               state[g][half(e), q, :], start=True, stop=True)
                        mm.then_inc(pred_full[k], 1)
                    if name == "new":
                        pe.wait_ge(const_in, 16)
                        if k == 0:
                            pe.wait_ge(invT_ready, now)
                        pe.wait_ge(u_ready[k], now)
                        for q, (b, hp) in enumerate(pair_of):
                            for e in range(2):
                                hd = hp * 2 + e
                                mm = pe.matmul(solo[1][half(k), q * P + DH * e:q * P + DH * e + DH], invT[half(k), e, q, :],
                                               v[half(k), b, hd * DH:(hd + 1) * DH], start=True, stop=True)
                        mm.then_inc(vn_full[k], 1)
                    if name == "state":
                        pe.wait_ge(const_in, 16)
                        if k == 0:
                            pe.wait_ge(rg_ready, now)
                        if k == 0:
                            pe.wait_ge(kg_ready, now)
                        pe.wait_ge(vn_ready[k], now)
                        for q in range(NP):
                            for e in range(2):
                                cols = slice(q * P + C * k, q * P + C * k + C)
                                pe.matmul(duo[0][half(e), 1, cols], state[g][half(e), q, :], rg[half(e), q, C * k:C * k + C], start=True, stop=True)
                                pe.matmul(duo[0][half(e), 0, cols], vn[half(k), q, e, :], intra[half(k), e, q, :], start=True, stop=True)
                                mm = pe.matmul(solo[0][half(e), q * DH:(q + 1) * DH], kg[half(k), q, e, :], vn[half(k), q, e, :], start=True, stop=True)
                        mm.then_inc(ds_full[k], 1)
                    if name == "attn_out":
                        pe.wait_ge(oT_ready, now)
                        for b in range(NB):
                            for hp in range(H // 2):
                                mm = pe.matmul(duo[1][:, 0, b * D:(b + 1) * D], oT[:, b * (H // 2) + hp, :], wr_sb[:, hp, :],
                                               start=hp == 0, stop=hp == H // 2 - 1)
                        mm.then_inc(ao_full, 1)
                    if name == "ln2":
                        pe.wait_ge(xn2_ready, n)
                        for kt in range(KT):
                            for b in range(NB):
                                mm = pe.transpose(solo[1][:, (kt * NB + b) * P:(kt * NB + b + 1) * P], xn2[:, b, kt * P:(kt + 1) * P], ident)
                        mm.then_inc(h2T_full, 1)

                walk(part, now_on)

            first_step(lambda *args: step(False, *args))
            pe.wait_ge(flag_col, 1)
            pe.transpose(mlp[1][0:1, 0:P], any_diff[:], ident).then_inc(flag_row, 1)
            pe.wait_ge(flag_set, 1)
            any_low = pe.value_load(flag_i[0:1, 0:1], min_val=0, max_val=1)
            with pe.If(any_low > 0):
                program(True)
            with pe.Else():
                program(False)


INPUTS = ("x", "wts", "wv", "wr", "wmod", "cT", "scales", "s3", "decay", "const", "sel")


def kernel(**inputs):
    import concourse.bacc as bacc
    from concourse.bass_utils import run_bass_kernel_spmd

    a = {k[3:]: np.asarray(v) for k, v in inputs.items()}

    def turned(w):
        o, i = w.shape
        return w.reshape(o // P, P, i // P, P).transpose(3, 0, 2, 1).reshape(P, -1, P)

    w3 = a["ffn_w3_w"].reshape(KT, P, HK, P).transpose(3, 2, 0, 1).reshape(P, -1, P)
    blocks = np.concatenate([turned(a["ffn_w1_w"]), turned(a["ffn_w2_w"]), turned(a["ffn_h1_w"]), turned(a["ffn_h2_w"]), w3], 1)
    rows = lambda w: w.reshape(KT, P, -1).transpose(1, 0, 2)
    pair = lambda z: np.repeat(z.reshape(H // 2, 2).T, C, axis=0)
    arrays = {
        "x": a["attn_out"],
        "wts": blocks.reshape(P, SLOTS, SLOT * P).transpose(1, 0, 2),
        "wv": rows(a["attn_Ww"].T),
        "wr": rows(a["attn_Wr"].T),
        "wmod": rows(a["wmod"]),
        "cT": rows(a["c"].T),
        "scales": np.stack([a["ffn_" + k].reshape(HK, P).T for k in ("w1_s", "w2_s", "h1_s", "h2_s")], 1),
        "s3": np.repeat(a["ffn_w3_s"][None], B, axis=0),
        "decay": np.concatenate([pair(a["attn_decay"]), np.repeat(a["attn_decay"].reshape(H // 2, 2).T.reshape(1, H), P, axis=0),
                                 pair(a["attn_log_alpha"])], 1),
        "const": constants(),
        "sel": selectors(),
    }
    arrays = {k: np.ascontiguousarray(v) for k, v in arrays.items()}
    nc = bacc.Bacc("TRN2", target_bir_lowering=False, num_devices=1, dynamic_dma_scratch_size=1024)
    aps = [nc.dram_tensor(f"in_{k}", arrays[k].shape, F32, kind="ExternalInput").ap() for k in INPUTS]
    out = nc.dram_tensor("out_y", (B, T, D), F32, kind="ExternalOutput").ap()
    adaln_block(nc, *aps, out)
    r = run_bass_kernel_spmd(nc, [{f"in_{k}": arrays[k] for k in INPUTS}], core_ids=[0])
    return r.results[0]["out_y"]
```
